# Optimizing a Trainium2 kernel written in Bass

```python
import numpy as np
import jax
import jax.numpy as jnp

def _softmax(x, axis=-1):
    return jax.nn.softmax(x, axis=axis)

def _gelu(x):
    return jax.nn.gelu(x, approximate=True)

def _silu(x):
    return jax.nn.silu(x)

def _sigmoid(x):
    return jax.nn.sigmoid(x)

def _layernorm(x, axis=-1, eps=1e-05):
    m = jnp.mean(x, axis=axis, keepdims=True)
    v = jnp.var(x, axis=axis, keepdims=True)
    return (x - m) / jnp.sqrt(v + eps)

def _scatter_add(tgt, idx, src, axis=0):
    return tgt.at[idx].add(src)

def _segment_sum(src, seg, n):
    return jax.ops.segment_sum(src, seg, n)
kernel_name = 'mk_seq_preln_d1_jaxref_r4_00af31'

def setup_inputs(seed: int=0):
    np.random.seed(seed)
    _w = jnp.asarray

    def _L0_attn_setup():
        import jax, jax.numpy as jnp
        import numpy as np
        EMBED_DIM = 256
        NUM_HEADS = 16
        HEAD_DIM = EMBED_DIM // NUM_HEADS
        INV_SCALE = float(HEAD_DIM) ** 0.5
        key = jax.random.key(seed)
        ks = jax.random.split(key, 9)
        E = EMBED_DIM
        s = 1.0 / np.sqrt(E)
        x = jax.random.normal(ks[0], (2, 512, E), dtype=jnp.float32)
        Wq = jax.random.uniform(ks[1], (E, E), jnp.float32, -s, s)
        bq = jax.random.uniform(ks[2], (E,), jnp.float32, -s, s)
        Wk = jax.random.uniform(ks[3], (E, E), jnp.float32, -s, s)
        bk = jax.random.uniform(ks[4], (E,), jnp.float32, -s, s)
        Wv = jax.random.uniform(ks[5], (E, E), jnp.float32, -s, s)
        bv = jax.random.uniform(ks[6], (E,), jnp.float32, -s, s)
        Wo = jax.random.uniform(ks[7], (E, E), jnp.float32, -s, s)
        bo = jax.random.uniform(ks[8], (E,), jnp.float32, -s, s)
        return {'x': x, 'Wq': Wq, 'bq': bq, 'Wk': Wk, 'bk': bk, 'Wv': Wv, 'bv': bv, 'Wo': Wo, 'bo': bo}
    _L0_attn_in = _L0_attn_setup()

    def _L0_ffn_setup():
        import jax, jax.numpy as jnp
        import numpy as np
        DIM = 256

        def _reference_tuple_inner(x, W_r, W_k, W_v, mu_r, mu_k):
            B, T, C = x.shape
            x_prev = jnp.concatenate([jnp.zeros((B, 1, C), x.dtype), x[:, :-1, :]], axis=1)
            xr = mu_r * x + (1.0 - mu_r) * x_prev
            xk = mu_k * x + (1.0 - mu_k) * x_prev
            r = jax.nn.sigmoid(jnp.einsum('btc,dc->btd', xr, W_r))
            k = jnp.einsum('btc,dc->btd', xk, W_k)
            k_act = jnp.square(jax.nn.relu(k))
            out = r * jnp.einsum('btc,dc->btd', k_act, W_v)
            new_state = x[:, -1, :]
            return (out, new_state)
        key = jax.random.key(seed)
        ks = jax.random.split(key, 6)
        B, T, C = (8, 512, DIM)
        x = jax.random.normal(ks[0], (B, T, C), dtype=jnp.float32)
        s = 1.0 / np.sqrt(C)
        W_r = jax.random.uniform(ks[1], (C, C), jnp.float32, -s, s)
        W_k = jax.random.uniform(ks[2], (C, C), jnp.float32, -s, s)
        W_v = jax.random.uniform(ks[3], (C, C), jnp.float32, -s, s)
        mu_r = jax.random.uniform(ks[4], (C,), jnp.float32)
        mu_k = jax.random.uniform(ks[5], (C,), jnp.float32)
        return {'x': x, 'W_r': W_r, 'W_k': W_k, 'W_v': W_v, 'mu_r': mu_r, 'mu_k': mu_k}
    _L0_ffn_in = _L0_ffn_setup()
    _d = {'L0_attn_x': _L0_attn_in['x'], 'L0_attn_Wq': _L0_attn_in['Wq'], 'L0_attn_bq': _L0_attn_in['bq'], 'L0_attn_Wk': _L0_attn_in['Wk'], 'L0_attn_bk': _L0_attn_in['bk'], 'L0_attn_Wv': _L0_attn_in['Wv'], 'L0_attn_bv': _L0_attn_in['bv'], 'L0_attn_Wo': _L0_attn_in['Wo'], 'L0_attn_bo': _L0_attn_in['bo'], 'L0_ffn_W_r': _L0_ffn_in['W_r'], 'L0_ffn_W_k': _L0_ffn_in['W_k'], 'L0_ffn_W_v': _L0_ffn_in['W_v'], 'L0_ffn_mu_r': _L0_ffn_in['mu_r'], 'L0_ffn_mu_k': _L0_ffn_in['mu_k']}
    _x0 = _d['L0_attn_x']
    _d['L0_attn_x'] = jax.random.normal(jax.random.fold_in(jax.random.key(seed), 1), (4, 2048, 256), dtype=_x0.dtype)
    del _x0
    return _d

def reference(L0_attn_x, L0_attn_Wq, L0_attn_bq, L0_attn_Wk, L0_attn_bk, L0_attn_Wv, L0_attn_bv, L0_attn_Wo, L0_attn_bo, L0_ffn_W_r, L0_ffn_W_k, L0_ffn_W_v, L0_ffn_mu_r, L0_ffn_mu_k):

    def _L0_attn_ref(x, Wq, bq, Wk, bk, Wv, bv, Wo, bo):
        import jax, jax.numpy as jnp
        import numpy as np
        EMBED_DIM = 256
        NUM_HEADS = 16
        HEAD_DIM = EMBED_DIM // NUM_HEADS
        INV_SCALE = float(HEAD_DIM) ** 0.5
        B, N, C = x.shape
        H, D = (NUM_HEADS, HEAD_DIM)
        q = (x @ Wq.T + bq).reshape(B, N, H, D).transpose(0, 2, 1, 3)
        k = (x @ Wk.T + bk).reshape(B, N, H, D).transpose(0, 2, 1, 3)
        v = (x @ Wv.T + bv).reshape(B, N, H, D).transpose(0, 2, 1, 3)
        logits = jnp.einsum('bhnd,bhmd->bhnm', q, k) * INV_SCALE
        attn = jax.nn.softmax(logits, axis=-1)
        h = jnp.einsum('bhnm,bhmd->bhnd', attn, v)
        concat_h = h.transpose(0, 2, 1, 3).reshape(B, N, C)
        return concat_h @ Wo.T + bo

    def _L0_ffn_ref(x, W_r, W_k, W_v, mu_r, mu_k):
        import jax, jax.numpy as jnp
        import numpy as np
        DIM = 256

        def _reference_tuple_inner(x, W_r, W_k, W_v, mu_r, mu_k):
            B, T, C = x.shape
            x_prev = jnp.concatenate([jnp.zeros((B, 1, C), x.dtype), x[:, :-1, :]], axis=1)
            xr = mu_r * x + (1.0 - mu_r) * x_prev
            xk = mu_k * x + (1.0 - mu_k) * x_prev
            r = jax.nn.sigmoid(jnp.einsum('btc,dc->btd', xr, W_r))
            k = jnp.einsum('btc,dc->btd', xk, W_k)
            k_act = jnp.square(jax.nn.relu(k))
            out = r * jnp.einsum('btc,dc->btd', k_act, W_v)
            new_state = x[:, -1, :]
            return (out, new_state)
        return _reference_tuple_inner(x, W_r, W_k, W_v, mu_r, mu_k)[0]
    x = L0_attn_x
    x = x + _L0_attn_ref(_layernorm(x, axis=-1), L0_attn_Wq, L0_attn_bq, L0_attn_Wk, L0_attn_bk, L0_attn_Wv, L0_attn_bv, L0_attn_Wo, L0_attn_bo)
    x = x + _L0_ffn_ref(_layernorm(x, axis=-1), L0_ffn_W_r, L0_ffn_W_k, L0_ffn_W_v, L0_ffn_mu_r, L0_ffn_mu_k)
    return x

_drawn_inputs = setup_inputs


def setup_inputs(seed=0):
    import zlib

    import numpy as np

    out = dict(_drawn_inputs(seed))
    spreads = {}
    factors = {'L0_attn_bk': 8.0, 'L0_attn_bv': 2.824, 'L0_ffn_W_r': 3.229, 'L0_ffn_mu_r': 6.508}
    for name, (base, spread) in spreads.items():
        noise = np.random.default_rng([zlib.crc32(name.encode()), seed]).standard_normal(out[name].shape)
        drawn = base * np.exp(spread * noise) if base else spread * noise
        out[name] = jnp.asarray(drawn.astype(out[name].dtype))
    for name, factor in factors.items():
        out[name] = (out[name] * factor).astype(out[name].dtype)
    return out
```

```python
from contextlib import ExitStack

import concourse.bass as bass
from concourse import mybir

F32 = mybir.dt.float32
BF16 = mybir.dt.bfloat16
I32 = mybir.dt.int32
ALU = mybir.AluOpType
ACT = mybir.ActivationFunctionType
AX = mybir.AxisListType

P = 128
B, N, C, H = 4, 2048, 256, 16
D = C // H
KH = C // P
TB = 512
TT = TB // P
BLOCKS = B * N // TB
BPB = N // TB
G = 4
UNITS = B * H // G
QB = N // TB
ITS = UNITS * QB
CH = N // P
KB = N // TB
PARTS = 3
PAIRS = ((0, 0), (1, 0), (2, 0), (0, 1), (1, 1), (0, 2))
SR = len(PAIRS) * D
MR = SR + PARTS
QRING = 4
SCALE = float(D) ** 0.5
EPS = 1e-5
RSQRT_SEED = float(0x5F3759DF)
DMA = 16


class Steps:

    CREDIT = 2

    def __init__(self, sem, names):
        self.sem, self.names = sem, names

    def start(self, eng):
        eng.sem_inc(self.sem, self.CREDIT * len(self.names))

    def done(self, ins):
        ins.then_inc(self.sem, 1)

    def done_alone(self, eng):
        eng.sem_inc(self.sem, 1)

    def value(self, block, name):
        return (block + self.CREDIT) * len(self.names) + self.names.index(name) + 1

    def wait(self, eng, block, name):
        eng.wait_ge(self.sem, self.value(block, name))


LN_STEPS = ([f"stats{t}" for t in range(TT)] + ["all stats"] + [f"meanvar{t}" for t in range(TT)] +
            ["eps", "shift", "seed"] + [f"newton{n}{s}" for n in range(3) for s in "abcd"] +
            [f"norm{t}" for t in range(TT)])


def settle(eng, sem):
    eng.sem_inc(sem, 1)


def layernorm(dve, steps, blk, x, xn, stats, mv, w):
    ve, half, y, t, z = (w[:, n, :] for n in range(5))
    for n in range(TT):
        steps.done(dve.bn_stats(stats[:, n, :], x[:, n, :]))
    steps.wait(dve, blk, f"stats{TT - 1}")
    steps.done_alone(dve)
    for n in range(TT):
        steps.done(dve.bn_aggr(mv[:, n, :], stats[:, n, :]))
    steps.wait(dve, blk, f"meanvar{TT - 1}")
    steps.done(dve.tensor_scalar(ve, mv[:, :, 1], EPS, None, ALU.add))
    steps.wait(dve, blk, "eps")
    steps.done(dve.tensor_scalar(half.bitcast(I32), ve.bitcast(I32), 1, None, ALU.logical_shift_right))
    steps.wait(dve, blk, "shift")
    steps.done(dve.tensor_scalar(y.bitcast(I32), half.bitcast(I32), -1.0, RSQRT_SEED, ALU.mult, ALU.add))
    last = "seed"
    for n in range(3):
        steps.wait(dve, blk, last)
        steps.done(dve.tensor_tensor(t, y, y, ALU.mult))
        steps.wait(dve, blk, f"newton{n}a")
        steps.done(dve.tensor_tensor(z, t, ve, ALU.mult))
        steps.wait(dve, blk, f"newton{n}b")
        steps.done(dve.tensor_scalar(t, z, -0.5, 1.5, ALU.mult, ALU.add))
        steps.wait(dve, blk, f"newton{n}c")
        steps.done(dve.tensor_tensor(y, y, t, ALU.mult))
        last = f"newton{n}d"
    steps.wait(dve, blk, last)
    for n in range(TT):
        steps.done(dve.tensor_scalar(xn[:, n, :], x[:, n, :], mv[:, n, 0:1], y[:, n:n + 1],
                                     ALU.subtract, ALU.mult))


def make_identity(pool, ident, sem):
    pool.memset(ident[:, :], 0.0).then_inc(sem, 1)
    pool.wait_ge(sem, 1)
    pool.affine_select(out=ident[:, :], in_=ident[:, :], compare_op=ALU.not_equal, fill=1.0, base=0,
                       pattern=[[-1, P]], channel_multiplier=1).then_inc(sem, 1)


def stage_project(nc, psum, x, wqT, wkT, wvT, bq, bk, q_d, k_d, v_d):
    with ExitStack() as ctx:
        def sb(name, shape, dt):
            return ctx.enter_context(nc.sbuf_tensor(name, shape, dt))

        def sem(name):
            return ctx.enter_context(nc.semaphore(name))

        ident = sb("p_ident", [P, P], F32)
        w_sb = {n: sb(f"p_w{n}", [P, KH, C], F32) for n in "qkv"}
        bias = {n: sb(f"p_b{n}", [P, KH], F32) for n in "qk"}
        x_sb = [sb(f"p_x{s}", [P, TT, C], F32) for s in range(2)]
        xn = [sb(f"p_xn{s}", [P, TT, C], F32) for s in range(2)]
        xnT = [sb(f"p_xnT{s}", [P, KH, TB], F32) for s in range(2)]
        full = [sb(f"p_full{s}", [P, 4, TB], F32) for s in range(2)]
        rest = [sb(f"p_rest{s}", [P, 4, TB], F32) for s in range(2)]
        parts = [sb(f"p_parts{s}", [P, 4, PARTS, TB], BF16) for s in range(2)]
        v_sb = [sb(f"p_v{s}", [P, TT, C], F32) for s in range(2)]
        stats = sb("p_stats", [P, TT, 6], F32)
        mv = sb("p_mv", [P, TT, 2], F32)
        work = sb("p_work", [P, 5, TT], F32)

        s_w = sem("p_s_w")
        s_id = sem("p_s_id")
        s_gate = sem("p_s_gate")
        s_x = [sem(f"p_s_x{s}") for s in range(2)]
        s_wr = [sem(f"p_s_wr{s}") for s in range(2)]
        jobs = [("q", 0), ("q", 1), ("k", 0), ("k", 1)]
        ln = Steps(sem("p_s_ln"), LN_STEPS)
        pe = Steps(sem("p_s_pe"), ["turned0", "turned1"] + [f"{n}{h}" for n, h in jobs] + ["v0", "v1"])
        act = Steps(sem("p_s_act"), ["xnT0", "xnT1"] +
                    [f"{s}{n}{h}" for n, h in jobs for s in ("full_", "part0_")] + ["v0", "v1"])
        spl = Steps(sem("p_s_spl"), [f"{s}{n}{h}" for n, h in jobs for s in ("rest_", "part1_", "part2_")])
        PER_SLOT = 4 * 8 + 4

        x_v = x.rearrange("b (m t p) c -> (b m) p t c", p=P, t=TT)
        block = ctx.enter_context(nc.Block())

        @block.sync
        def _(sp):
            for n, src in (("q", wqT), ("k", wkT), ("v", wvT)):
                sp.dma_start(w_sb[n][:, :, :], src.rearrange("(k p) n -> p k n", p=P)).then_inc(s_w, DMA)
            for n, src in (("q", bq), ("k", bk)):
                sp.dma_start(bias[n][:, :], src).then_inc(s_w, DMA)

            def load(s, blk, turn):
                sp.dma_start(x_sb[s][:, :, :], x_v[blk, :, :, :]).then_inc(s_x[s], DMA)

            def store(s, blk, turn):
                act.wait(sp, blk, "v1")
                settle(sp, s_gate)
                seq, tb = blk // BPB, blk % BPB
                for n in range(4):
                    sp.dma_start(v_d[seq * 4 + n, :, bass.ds(tb * TT, TT), :],
                                 v_sb[s][:, :, n * G * D:(n + 1) * G * D]).then_inc(s_wr[s], DMA)
                for j, (n, h) in enumerate(jobs):
                    spl.wait(sp, blk, f"part2_{n}{h}")
                    settle(sp, s_gate)
                    for e in range(P // D):
                        head = h * (P // D) + e
                        src = parts[s][e * D:(e + 1) * D, j, :, :]
                        if n == "q":
                            it = (seq * 4 + head // G) * QB + tb
                            dst = q_d[it, :, head % G, :].rearrange("(a d) t -> d a t", d=D)
                        else:
                            dst = k_d[seq * H + head, :, bass.ds(tb * TB, TB)].rearrange(
                                "(a d) t -> d a t", d=D)
                        sp.dma_start(dst, src).then_inc(s_wr[s], DMA)

            for s in range(2):
                sp.sem_inc(s_wr[s], DMA)
                load(s, s, 0)
            with sp.Fori(0, BLOCKS // 2 - 1) as turn:
                for s in range(2):
                    blk = turn * 2 + s
                    ln.wait(sp, blk, f"norm{TT - 1}")
                    settle(sp, s_gate)
                    load(s, blk + 2, turn)
                    store(s, blk, turn)
            for s in range(2):
                store(s, BLOCKS - 2 + s, BLOCKS // 2 - 1)
            for s in range(2):
                sp.wait_ge(s_wr[s], DMA * (PER_SLOT * (BLOCKS // 2) + 1))

        @block.gpsimd
        def _(pool):
            make_identity(pool, ident, s_id)

        @block.vector
        def _(dve):
            ln.start(dve)
            spl.start(dve)
            with dve.Fori(0, BLOCKS // 2) as turn:
                for s in range(2):
                    blk = turn * 2 + s
                    dve.wait_ge(s_x[s], DMA * (turn + 1))
                    layernorm(dve, ln, blk, x_sb[s], xn[s], stats, mv, work)
                    for j, (n, h) in enumerate(jobs):
                        act.wait(dve, blk, f"part0_{n}{h}")
                        spl.done(dve.tensor_tensor(rest[s][:, j, :], full[s][:, j, :],
                                                   parts[s][:, j, 0, :], ALU.subtract))
                        spl.wait(dve, blk, f"rest_{n}{h}")
                        spl.done(dve.tensor_copy(parts[s][:, j, 1, :], rest[s][:, j, :]))
                        spl.wait(dve, blk, f"part1_{n}{h}")
                        spl.done(dve.tensor_tensor(parts[s][:, j, 2, :], rest[s][:, j, :],
                                                   parts[s][:, j, 1, :], ALU.subtract))

        @block.tensor
        def _(te):
            pe.start(te)
            te.wait_ge(s_id, 2)
            te.wait_ge(s_w, DMA * 5)
            with te.Fori(0, BLOCKS // 2) as turn:
                for s in range(2):
                    blk = turn * 2 + s
                    te.wait_ge(ln.sem, ln.value(blk, f"norm{TT - 1}"))
                    for h in range(KH):
                        for t in range(TT):
                            m = te.transpose(psum[:, h, t * P:(t + 1) * P], xn[s][:, t, h * P:(h + 1) * P],
                                             ident[:, :])
                        pe.done(m)
                    act.wait(te, blk, "xnT1")
                    for j, (n, h) in enumerate(jobs):
                        for k in range(KH):
                            m = te.matmul(psum[:, 2 + j, :], w_sb[n][:, k, h * P:(h + 1) * P],
                                          xnT[s][:, k, :], start=(k == 0), stop=(k == KH - 1))
                        pe.done(m)
                    for t in range(TT):
                        o = psum[:, 6 + t // 2, (t % 2) * C:(t % 2 + 1) * C]
                        for k in range(KH):
                            m = te.matmul(o, xnT[s][:, k, t * P:(t + 1) * P], w_sb["v"][:, k, :],
                                          start=(k == 0), stop=(k == KH - 1))
                        if t % 2:
                            pe.done(m)

        @block.scalar
        def _(ac):
            act.start(ac)
            ac.wait_ge(s_w, DMA * 5)
            with ac.Fori(0, BLOCKS // 2) as turn:
                for s in range(2):
                    blk = turn * 2 + s
                    for h in range(KH):
                        pe.wait(ac, blk, f"turned{h}")
                        act.done(ac.copy(xnT[s][:, h, :], psum[:, h, :]))
                    ac.wait_ge(s_wr[s], DMA * (PER_SLOT * turn + 1))
                    for j, (n, h) in enumerate(jobs):
                        pe.wait(ac, blk, f"{n}{h}")
                        act.done(ac.activation(full[s][:, j, :], psum[:, 2 + j, :], ACT.Identity,
                                               bias=bias[n][:, h:h + 1]))
                        act.done(ac.activation(parts[s][:, j, 0, :], psum[:, 2 + j, :], ACT.Identity,
                                               bias=bias[n][:, h:h + 1]))
                    for t in range(0, TT, 2):
                        pe.wait(ac, blk, f"v{t // 2}")
                        act.done(ac.copy(v_sb[s][:, t:t + 2, :].rearrange("p t c -> p (t c)"),
                                         psum[:, 6 + t // 2, :]))


def stage_attend(nc, psum, q_d, k_d, v_d, num_d, den_d):
    LEAD = CH + 4
    AHEAD = LEAD - CH
    ST, O, SP, TR = 0, 4, 5, 7
    with ExitStack() as ctx:
        def sb(name, shape, dt):
            return ctx.enter_context(nc.sbuf_tensor(name, shape, dt))

        def sem(name):
            return ctx.enter_context(nc.semaphore(name))

        ks = sb("a_ks", [MR, 2, G, N], BF16)
        qs = sb("a_qs", [MR, QRING, G * TB], BF16)
        v_in = sb("a_vin", [P, 2, CH, G * D], F32)
        v_st = sb("a_vst", [P, CH, G, D + 1], F32)
        p_sb = sb("a_p", [P, 2, G, TB], F32)
        o_sb = sb("a_o", [P, TB], F32)
        ident = sb("a_ident", [P, P], BF16)
        mx = sb("a_mx", [P, G * TT, KB], F32)
        m = sb("a_m", [P, G * TT], F32)
        m_rest = sb("a_mrest", [P, G * TT], F32)
        m_parts = sb("a_mparts", [P, PARTS, G * TT], BF16)
        m_rows = sb("a_mrows", [PARTS * G * TT, P], BF16)

        s_id = sem("a_s_id")
        s_one = sem("a_s_one")
        s_k = sem("a_s_k")
        s_q = sem("a_s_q")
        s_v = sem("a_s_v")
        s_vc = sem("a_s_vc")
        s_st = sem("a_s_st")
        s_exp = sem("a_s_exp")
        s_sp = sem("a_s_sp")
        s_mx = sem("a_s_mx")
        s_ch = sem("a_s_ch")
        s_mt = sem("a_s_mt")
        s_mc = sem("a_s_mc")
        s_mr = sem("a_s_mr")
        s_pv = sem("a_s_pv")
        s_oe = sem("a_s_oe")
        s_out = sem("a_s_out")
        s_te, s_sp_gate = sem("a_s_te"), sem("a_s_gate")
        K_INC, Q_INC, V_INC = DMA * len(PAIRS), DMA * 3, DMA
        M_INC, OUT_INC = DMA * PARTS, DMA * 2 * G
        CHAIN = 5

        block = ctx.enter_context(nc.Block())

        @block.sync
        def _(sp):
            def load_k(piece):
                dst = ks[:, (piece // G) % 2, piece % G, :]
                for r, (_, a) in enumerate(PAIRS):
                    sp.dma_start(dst[r * D:(r + 1) * D, :], k_d[piece, a * D:(a + 1) * D, :]
                                 ).then_inc(s_k, DMA)

            def load_q(it):
                row = 0
                for n in (3, 2, 1):
                    sp.dma_start(qs[row:row + n * D, it % QRING, :].rearrange("p (g t) -> p g t", g=G),
                                 q_d[it, 0:n * D, :, :]).then_inc(s_q, DMA)
                    row += n * D

            def load_v(piece):
                c = (piece % G) * (CH // G)
                sp.dma_start(v_in[:, (piece // G) % 2, bass.ds(c, CH // G), :],
                             v_d[piece // G, :, bass.ds(c, CH // G), :]).then_inc(s_v, DMA)

            def rows(it):
                sp.wait_ge(s_mc, it + 1)
                settle(sp, s_sp_gate)
                for a in range(PARTS):
                    sp.dma_start(qs[SR + a:SR + a + 1, it % QRING, :].rearrange("o (n p) -> o n p", p=P),
                                 m_rows[a * G * TT:(a + 1) * G * TT, :]).then_inc(s_mr, DMA)

            def out(it):
                sp.wait_ge(s_oe, it + 2)
                settle(sp, s_sp_gate)
                seq, grp, qb = it // (G * QB), (it // QB) % G, it % QB
                for g in range(G):
                    for dst, row, n, w in ((num_d, 32 * g, D, D), (den_d, 32 * g + D, 1, 1)):
                        sp.dma_start(dst[bass.ds((grp * G + g) * w, n), bass.ds(seq * N + qb * TB, TB)],
                                     o_sb[row:row + n, :]).then_inc(s_out, DMA)

            def body(it, k, q):
                sp.wait_ge(s_st, it * 2 * CH + 1)
                sp.wait_ge(s_vc, it * CH + CH)
                settle(sp, s_sp_gate)
                if k:
                    load_k(it + G)
                    load_v(it + G)
                else:
                    sp.sem_inc(s_k, K_INC)
                    sp.sem_inc(s_v, V_INC)
                if q:
                    load_q(it + QRING - 1)
                else:
                    sp.sem_inc(s_q, Q_INC)
                if not isinstance(it, int) or it + 1 < ITS:
                    rows(it + 1)
                sp.wait_ge(s_k, K_INC * (it + G + 1))
                settle(sp, s_sp_gate)
                sp.wait_ge(s_v, V_INC * (it + G + 1))
                settle(sp, s_sp_gate)
                sp.wait_ge(s_q, Q_INC * (it + QRING))
                settle(sp, s_sp_gate)
                out(it)

            sp.sem_inc(s_out, DMA)
            for n in range(G):
                load_k(n)
                if n < QRING - 1:
                    load_q(n)
                load_v(n)
            rows(0)
            with sp.Fori(0, ITS - G) as it:
                body(it, True, True)
            for it in range(ITS - G, ITS):
                body(it, False, it + QRING - 1 < ITS)
            sp.wait_ge(s_out, DMA + OUT_INC * ITS)

        @block.gpsimd
        def _(pool):
            make_identity(pool, ident, s_id)
            pool.memset(v_st[:, :, :, D:D + 1], 1.0).then_inc(s_one, 1)

            def copy_v(it, c):
                pool.tensor_copy(v_st[:, c, :, 0:D],
                                 v_in[:, (it // QB) % 2, c, :].rearrange("p (g d) -> p g d", g=G)
                                 ).then_inc(s_vc, 1)

            pool.wait_ge(s_v, V_INC * G)
            for c in range(CH):
                copy_v(0, c)
            with pool.Fori(0, ITS - 1) as it:
                for c in range(CH):
                    if c in (0, CH - CH // G):
                        pool.wait_ge(s_v, V_INC * (it + G + (c > 0)))
                    pool.wait_ge(s_pv, it * CH + c + 3)
                    copy_v(it + 1, c)

        @block.scalar
        def _(ac):
            ac.sem_inc(s_exp, 2)
            ac.sem_inc(s_oe, 1)
            with ac.Fori(0, ITS) as it:
                for c in range(CH):
                    ac.wait_ge(s_pv, it * CH + c + 1)
                    for half in range(2):
                        ac.wait_ge(s_st, it * 2 * CH + 2 * c + half + 1)
                        ac.activation(p_sb[:, c % 2, 2 * half:2 * half + 2, :],
                                      psum[:, ST + 2 * half:ST + 2 * half + 2, :], ACT.Exp,
                                      scale=SCALE).then_inc(s_exp, 1)
                ac.wait_ge(s_pv, it * CH + CH + 2)
                ac.wait_ge(s_out, it * OUT_INC + DMA)
                for g in range(G):
                    e = ac.copy(o_sb[32 * g:32 * g + D + 1, :], psum[32 * g:32 * g + D + 1, O, :])
                e.then_inc(s_oe, 1)

        def stream(it, c):
            late = c >= CH - AHEAD
            return it + 1 + late, (c + AHEAD) % CH, (LEAD + CH * it + c) * KB

        @block.vector
        def _(dve):
            def reduce(pair, tile):
                for kb in range(KB):
                    dve.wait_ge(s_sp, tile + kb + 1)
                    dve.tensor_reduce(mx[:, pair, kb:kb + 1], psum[:, SP + kb % 2, :], AX.X, ALU.max
                                      ).then_inc(s_mx, 1)

            def chain(blk, tiles):
                dve.wait_ge(s_mx, tiles)
                dve.tensor_reduce(m[:, :], mx[:, :, :], AX.X, ALU.max).then_inc(s_ch, 1)
                dve.wait_ge(s_ch, blk * CHAIN + 1)
                dve.wait_ge(s_mt, blk) if not isinstance(blk, int) or blk else None
                dve.tensor_scalar(m_parts[:, 0, :], m[:, :], -1.0, None, ALU.mult).then_inc(s_ch, 1)
                dve.wait_ge(s_ch, blk * CHAIN + 2)
                dve.scalar_tensor_tensor(out=m_rest[:, :], in0=m[:, :], scalar=-1.0, in1=m_parts[:, 0, :],
                                         op0=ALU.mult, op1=ALU.subtract).then_inc(s_ch, 1)
                dve.wait_ge(s_ch, blk * CHAIN + 3)
                dve.tensor_copy(m_parts[:, 1, :], m_rest[:, :]).then_inc(s_ch, 1)
                dve.wait_ge(s_ch, blk * CHAIN + 4)
                dve.tensor_tensor(m_parts[:, 2, :], m_rest[:, :], m_parts[:, 1, :], ALU.subtract
                                  ).then_inc(s_ch, 1)

            def keep_rows(blk):
                dve.wait_ge(s_mt, blk + 1)
                dve.wait_ge(s_mr, M_INC * blk) if not isinstance(blk, int) or blk else None
                dve.tensor_copy(m_rows[:, :], psum[0:PARTS * G * TT, TR, 0:P // 2].bitcast(BF16)
                                ).then_inc(s_mc, 1)

            def body(it, steps):
                for c in steps:
                    blk, pair, tile = stream(it, c)
                    reduce(pair, tile)
                    if pair == CH - 1:
                        chain(blk, tile + KB)
                    if pair == 1 and c:
                        keep_rows(it + 1)

            for u in range(2):
                dve.memset(ks[SR:MR, u, :, :], 1.0).then_inc(s_one, 1)
            for pair in range(CH):
                reduce(pair, pair * KB)
            chain(0, CH * KB)
            keep_rows(0)
            for pair in range(AHEAD):
                reduce(pair, (CH + pair) * KB)
            with dve.Fori(0, ITS - 2) as it:
                body(it, range(CH))
            body(ITS - 2, range(CH - AHEAD))
            keep_rows(ITS - 1)

        @block.tensor
        def _(te):
            def scores(it, c, half):
                te.wait_ge(s_exp, it * 2 * CH + 2 * c + half + 1)
                for g in range(2 * half, 2 * half + 2):
                    mm = te.matmul(psum[:, ST + g, :], ks[0:MR, (it // QB) % 2, g, c * P:(c + 1) * P],
                                   qs[0:MR, it % QRING, g * TB:(g + 1) * TB], start=True, stop=True)
                mm.then_inc(s_st, 1)

            def peak(blk, pair, tile, kbs):
                for kb in kbs:
                    te.wait_ge(s_mx, tile + kb - 1) if not isinstance(tile, int) or tile + kb > 1 else None
                    te.matmul(psum[:, SP + kb % 2, :], qs[0:SR, blk % QRING, pair * P:(pair + 1) * P],
                              ks[0:SR, (blk // QB) % 2, pair // TT, kb * TB:(kb + 1) * TB],
                              start=True, stop=True).then_inc(s_sp, 1)

            def turn(blk):
                te.wait_ge(s_ch, CHAIN * (blk + 1))
                te.wait_ge(s_mc, blk) if not isinstance(blk, int) or blk else None
                settle(te, s_te)
                te.transpose(psum[0:PARTS * G * TT, TR, 0:P // 2].bitcast(BF16),
                             m_parts[:, :, :].rearrange("p a n -> p (a n)"), ident[:, :]).then_inc(s_mt, 1)

            def times_v(it, c):
                te.wait_ge(s_exp, it * 2 * CH + 2 * c + 4)
                te.wait_ge(s_vc, it * CH + c + 1)
                if c == 0:
                    te.wait_ge(s_oe, it + 1)
                for g in range(G):
                    mm = te.matmul(psum[32 * g:32 * g + D + 1, O, :], v_st[:, c, g, :],
                                   p_sb[:, c % 2, g, :], start=(c == 0), stop=(c == CH - 1))
                mm.then_inc(s_pv, 1)

            def body(it, steps):
                te.wait_ge(s_mr, M_INC * (it + 1))
                for c in range(CH):
                    blk, pair, tile = stream(it, c)
                    ahead = c < steps
                    if ahead and c == 0:
                        te.wait_ge(s_k, K_INC * (it + G))
                    if ahead and pair == 3 * TT:
                        te.wait_ge(s_k, K_INC * (it + G + 1))
                    if ahead and pair == 0:
                        te.wait_ge(s_q, Q_INC * (it + 3))
                    scores(it, c, 0)
                    if ahead:
                        peak(blk, pair, tile, (0, 1))
                    scores(it, c, 1)
                    if ahead:
                        peak(blk, pair, tile, (2,))
                    if c:
                        times_v(it, c - 1)
                    if ahead:
                        peak(blk, pair, tile, (3,))
                    if steps and c == CH - AHEAD:
                        turn(it + 1)
                times_v(it, CH - 1)

            te.sem_inc(s_pv, 2)
            te.wait_ge(s_id, 2)
            te.wait_ge(s_one, 3)
            te.wait_ge(s_k, K_INC * G)
            te.wait_ge(s_q, Q_INC * (QRING - 1))
            for pair in range(CH):
                peak(0, pair, pair * KB, range(KB))
            turn(0)
            for pair in range(AHEAD):
                peak(1, pair, (CH + pair) * KB, range(KB))
            with te.Fori(0, ITS - 2) as it:
                body(it, CH)
            body(ITS - 2, CH - AHEAD)
            body(ITS - 1, 0)


def stage_invert(nc, den_d, rden_d):
    W = H * B * N // P
    with ExitStack() as ctx:
        d = ctx.enter_context(nc.sbuf_tensor("i_den", [P, W], F32))
        r = ctx.enter_context(nc.sbuf_tensor("i_rden", [P, W], F32))
        s_in, s_r, s_o = (ctx.enter_context(nc.semaphore(f"i_s_{n}")) for n in ("in", "r", "out"))
        block = ctx.enter_context(nc.Block())

        @block.sync
        def _(sp):
            sp.dma_start(d[:, :], den_d.rearrange("h (a w) -> (h a) w", w=W)).then_inc(s_in, DMA)
            sp.wait_ge(s_r, 1)
            sp.dma_start(rden_d.rearrange("h (a w) -> (h a) w", w=W), r[:, :]).then_inc(s_o, DMA)
            sp.wait_ge(s_o, DMA)

        @block.vector
        def _(dve):
            dve.wait_ge(s_in, DMA)
            dve.reciprocal(r[:, :], d[:, :]).then_inc(s_r, 1)


def stage_mix(nc, psum, x, num_d, rden_d, bv, woT, bo, wrT, wkT, wvT, mu_r, mu_k, out):
    with ExitStack() as ctx:
        def sb(name, shape, dt):
            return ctx.enter_context(nc.sbuf_tensor(name, shape, dt))

        def sem(name):
            return ctx.enter_context(nc.semaphore(name))

        def two(name, shape):
            return [sb(f"m_{name}{s}", shape, F32) for s in range(2)]

        ident = sb("m_ident", [P, P], F32)
        w_sb = {n: sb(f"m_w{n}", [P, KH, C], F32) for n in "orkv"}
        col = {n: sb(f"m_{n}", [P, KH], F32) for n in ("bv", "mr", "mk")}
        bo_sb = sb("m_bo", [P, C], F32)
        x_sb, x1 = two("x", [P, TT, C]), two("x1", [P, TT, C])
        num, rden, hT = two("num", [P, KH, TB]), two("rden", [P, KH, TB]), two("hT", [P, KH, TB])
        xn = sb("m_xn", [P, TT, C], F32)
        xT = two("xT", [P, KH, TB + 1])
        diff = sb("m_diff", [P, KH, TB], F32)
        xr, xk = two("xr", [P, KH, TB]), two("xk", [P, KH, TB])
        kr, ka = sb("m_kr", [P, KH, TB], F32), sb("m_ka", [P, KH, TB], F32)
        gate = two("gate", [P, TT, C])
        y = two("y", [P, TT, C])
        stats = sb("m_stats", [P, TT, 6], F32)
        mv = sb("m_mv", [P, TT, 2], F32)
        work = sb("m_work", [P, 5, TT], F32)

        s_w, s_id, s_gate = sem("m_s_w"), sem("m_s_id"), sem("m_s_gate")
        s_in = [sem(f"m_s_in{s}") for s in range(2)]
        s_out = [sem(f"m_s_out{s}") for s in range(2)]
        HH = H // KH
        N_IN = (HH + 2) * KH
        ln = Steps(sem("m_s_ln"), ["x1"] + LN_STEPS)
        pf = Steps(sem("m_s_pf"), ["proj", "turned0", "turned1"])
        pb_ = Steps(sem("m_s_pb"), ["k", "r", "v"])
        gf = Steps(sem("m_s_gf"), ["h0", "h1", "xb"])
        gb = Steps(sem("m_s_gb"), ["sq", "y"])
        af = Steps(sem("m_s_af"), ["bias0", "bias1", "xT0", "xT1"])
        ab = Steps(sem("m_s_ab"), ["relu", "gate"])
        vb = Steps(sem("m_s_vb"), ["prev", "diff", "xk0", "xk1", "xr0", "xr1"])
        vy = Steps(sem("m_s_vy"), ["gated"])
        NW = 4 + 3 + 1

        x_v = x.rearrange("b (m t p) c -> (b m) p t c", p=P, t=TT)
        out_v = out.rearrange("b (m t p) c -> (b m) p t c", p=P, t=TT)
        block = ctx.enter_context(nc.Block())

        def turns(eng, front, back):
            def one(first, last):
                for n in range(BPB):
                    if not (last and n == BPB - 1):
                        front(first + n + 1, n + 1)
                    back(first + n, n)
            front(0, 0)
            with eng.Fori(0, B - 1) as seq:
                one(seq * BPB, False)
            one((B - 1) * BPB, True)

        def uses(blk):
            return blk // 2

        @block.sync
        def _(sp):
            for n, src in (("o", woT), ("r", wrT), ("k", wkT), ("v", wvT)):
                sp.dma_start(w_sb[n][:, :, :], src.rearrange("(k p) n -> p k n", p=P)).then_inc(s_w, DMA)
            for n, src in (("bv", bv), ("mr", mu_r), ("mk", mu_k)):
                sp.dma_start(col[n][:, :], src).then_inc(s_w, DMA)
            sp.dma_start(bo_sb[:, :], bo.rearrange("(o c) -> o c", o=1).to_broadcast([P, C])
                         ).then_inc(s_w, DMA)

            def front(blk, n):
                s = n % 2
                gf.wait(sp, blk - 2, "xb")
                ln.wait(sp, blk - 2, "x1")
                settle(sp, s_gate)
                tok = bass.ds(blk * TB, TB)
                for k in range(KH):
                    sp.dma_start(num[s][:, k, :], num_d[k * P:(k + 1) * P, tok]).then_inc(s_in[s], DMA)
                    for h in range(HH):
                        sp.dma_start(rden[s][h * D:(h + 1) * D, k, :],
                                     rden_d[k * HH + h:k * HH + h + 1, tok].to_broadcast([D, TB])
                                     ).then_inc(s_in[s], DMA)
                    sp.dma_start(x_sb[s][:, 2 * k:2 * k + 2, :], x_v[blk, :, 2 * k:2 * k + 2, :]
                                 ).then_inc(s_in[s], DMA)

            def back(blk, n):
                gb.wait(sp, blk, "y")
                settle(sp, s_gate)
                sp.dma_start(out_v[blk, :, :, :], y[n % 2][:, :, :]).then_inc(s_out[n % 2], DMA)

            for s in range(2):
                sp.sem_inc(s_out[s], DMA)
            turns(sp, front, back)
            for s in range(2):
                sp.wait_ge(s_out[s], DMA * (BLOCKS // 2 + 1))

        @block.gpsimd
        def _(pool):
            gf.start(pool)
            gb.start(pool)
            make_identity(pool, ident, s_id)
            pool.wait_ge(s_w, DMA * NW)

            def front(blk, n):
                s = n % 2
                pool.wait_ge(s_in[s], DMA * N_IN * (uses(blk) + 1))
                for k in range(KH):
                    pf.wait(pool, blk - 2, "proj")
                    gf.done(pool.tensor_tensor(hT[s][:, k, :], num[s][:, k, :], rden[s][:, k, :], ALU.mult))
                gf.done(pool.tensor_tensor(x_sb[s][:, :, :], x_sb[s][:, :, :],
                                           bo_sb[:, :].unsqueeze(1).to_broadcast([P, TT, C]), ALU.add))

            def back(blk, n):
                s = n % 2
                ab.wait(pool, blk, "relu")
                pb_.wait(pool, blk - 1, "v")
                gb.done(pool.tensor_tensor(ka[:, :, :], kr[:, :, :], kr[:, :, :], ALU.mult))
                vy.wait(pool, blk, "gated")
                gb.done(pool.tensor_tensor(y[s][:, :, :], y[s][:, :, :], x1[s][:, :, :], ALU.add))

            turns(pool, front, back)

        @block.scalar
        def _(ac):
            af.start(ac)
            ab.start(ac)
            ac.wait_ge(s_w, DMA * NW)

            def front(blk, n):
                s = n % 2
                for k in range(KH):
                    gf.wait(ac, blk, f"h{k}")
                    af.done(ac.activation(hT[s][:, k, :], hT[s][:, k, :], ACT.Identity,
                                          bias=col["bv"][:, k:k + 1]))
                for k in range(KH):
                    pf.wait(ac, blk, f"turned{k}")
                    vb.wait(ac, blk - 1, "prev")
                    af.done(ac.copy(xT[s][:, k, 1:TB + 1], psum[:, 2 + k, :]))

            def back(blk, n):
                s = n % 2
                pb_.wait(ac, blk, "k")
                gb.wait(ac, blk - 1, "sq")
                ab.done(ac.activation(kr[:, :, :], psum[:, 4:6, :], ACT.Relu))
                pb_.wait(ac, blk, "r")
                vy.wait(ac, blk - 2, "gated")
                ab.done(ac.activation(gate[s][:, :, :].rearrange("p t c -> p (t c)"),
                                      psum[:, 6:8, :].rearrange("p a c -> p (a c)"), ACT.Sigmoid))

            turns(ac, front, back)

        @block.vector
        def _(dve):
            for steps in (ln, vb, vy):
                steps.start(dve)
            dve.wait_ge(s_w, DMA * NW)

            def front(blk, n):
                s = n % 2
                pf.wait(dve, blk, "proj")
                gf.wait(dve, blk, "xb")
                gb.wait(dve, blk - 2, "y")
                ln.done(dve.tensor_tensor(x1[s][:, :, :].rearrange("p t c -> p (t c)"),
                                          psum[:, 0:2, :].rearrange("p a c -> p (a c)"),
                                          x_sb[s][:, :, :].rearrange("p t c -> p (t c)"), ALU.add))
                ln.wait(dve, blk, "x1")
                pf.wait(dve, blk - 1, "turned1")
                layernorm(dve, ln, blk, x1[s], xn, stats, mv, work)

            def back(blk, n):
                s = n % 2
                af.wait(dve, blk, "xT1")
                if n % BPB == 0:
                    vb.done(dve.memset(xT[s][:, :, 0:1], 0.0))
                else:
                    vb.done(dve.tensor_copy(xT[s][:, :, 0:1], xT[1 - s][:, :, TB:TB + 1]))
                vb.wait(dve, blk, "prev")
                vb.done(dve.tensor_tensor(diff[:, :, :], xT[s][:, :, 1:TB + 1], xT[s][:, :, 0:TB],
                                          ALU.subtract))
                vb.wait(dve, blk, "diff")
                pb_.wait(dve, blk - 2, "r")
                for name, dst, mu in (("xk", xk, "mk"), ("xr", xr, "mr")):
                    for k in range(KH):
                        vb.done(dve.scalar_tensor_tensor(out=dst[s][:, k, :], in0=diff[:, k, :],
                                                         scalar=col[mu][:, k:k + 1], in1=xT[s][:, k, 0:TB],
                                                         op0=ALU.mult, op1=ALU.add))
                pb_.wait(dve, blk, "v")
                ab.wait(dve, blk, "gate")
                dve.wait_ge(s_out[s], DMA * (uses(blk) + 1))
                vy.done(dve.tensor_tensor(y[s][:, :, :].rearrange("p t c -> p (t c)"),
                                          psum[:, 4:6, :].rearrange("p a c -> p (a c)"),
                                          gate[s][:, :, :].rearrange("p t c -> p (t c)"), ALU.mult))

            turns(dve, front, back)

        @block.tensor
        def _(te):
            pf.start(te)
            pb_.start(te)
            te.wait_ge(s_w, DMA * NW)
            te.wait_ge(s_id, 2)

            def by_token(bank, lhsT, w, steps):
                for t in range(TT):
                    for k in range(KH):
                        mm = te.matmul(psum[:, bank + t // 2, (t % 2) * C:(t % 2 + 1) * C],
                                       lhsT[:, k, t * P:(t + 1) * P], w[:, k, :],
                                       start=(k == 0), stop=(k == KH - 1))
                steps.done(mm)

            def proj(blk, n):
                af.wait(te, blk, "bias1")
                ln.wait(te, blk - 1, "x1")
                by_token(0, hT[n % 2], w_sb["o"], pf)

            def turned(blk, n):
                ln.wait(te, blk, f"norm{TT - 1}")
                af.wait(te, blk - 1, "xT1")
                for h in range(KH):
                    for t in range(TT):
                        mm = te.transpose(psum[:, 2 + h, t * P:(t + 1) * P], xn[:, t, h * P:(h + 1) * P],
                                          ident[:, :])
                    pf.done(mm)

            def products(blk, n):
                s = n % 2
                vb.wait(te, blk, "xk1")
                vy.wait(te, blk - 1, "gated")
                for h in range(KH):
                    for k in range(KH):
                        mm = te.matmul(psum[:, 4 + h, :], w_sb["k"][:, k, h * P:(h + 1) * P], xk[s][:, k, :],
                                       start=(k == 0), stop=(k == KH - 1))
                pb_.done(mm)
                vb.wait(te, blk, "xr1")
                ab.wait(te, blk - 1, "gate")
                by_token(6, xr[s], w_sb["r"], pb_)

            def value(blk, n):
                gb.wait(te, blk, "sq")
                by_token(4, ka, w_sb["v"], pb_)

            pending = []

            def front(blk, n):
                proj(blk, n)
                if isinstance(blk, int) and blk == 0:
                    turned(blk, n)
                else:
                    pending.append((blk, n))

            def back(blk, n):
                products(blk, n)
                if pending:
                    turned(*pending.pop())
                value(blk, n)

            turns(te, front, back)


def build(nc, a):
    dram = nc.dram_tensor
    q_d = dram("q_parts", (ITS, PARTS * D, G, TB), BF16).ap()
    k_d = dram("k_parts", (B * H, PARTS * D, N), BF16).ap()
    v_d = dram("v_rows", (UNITS, P, CH, G * D), F32).ap()
    num_d = dram("numerators", (C, B * N), F32).ap()
    den_d = dram("denominators", (H, B * N), F32).ap()
    rden_d = dram("inverse_denominators", (H, B * N), F32).ap()
    with nc.psum_tensor("psum", [P, 8, TB], F32) as psum:
        stage_project(nc, psum, a["x"], a["wqT"], a["wkT"], a["wvT"], a["bq"], a["bk"], q_d, k_d, v_d)
        stage_attend(nc, psum, q_d, k_d, v_d, num_d, den_d)
        stage_invert(nc, den_d, rden_d)
        stage_mix(nc, psum, a["x"], num_d, rden_d, a["bv"], a["woT"], a["bo"], a["fwrT"], a["fwkT"],
                  a["fwvT"], a["mu_r"], a["mu_k"], a["out"])


def kernel(L0_attn_x, L0_attn_Wq, L0_attn_bq, L0_attn_Wk, L0_attn_bk, L0_attn_Wv, L0_attn_bv,
           L0_attn_Wo, L0_attn_bo, L0_ffn_W_r, L0_ffn_W_k, L0_ffn_W_v, L0_ffn_mu_r, L0_ffn_mu_k):
    import concourse.bacc as bacc
    import numpy as np
    from concourse.bass_utils import run_bass_kernel_spmd

    turned = {"wqT": L0_attn_Wq, "wkT": L0_attn_Wk, "wvT": L0_attn_Wv, "woT": L0_attn_Wo,
              "fwrT": L0_ffn_W_r, "fwkT": L0_ffn_W_k, "fwvT": L0_ffn_W_v}
    arrays = {n: np.ascontiguousarray(np.asarray(w).T) for n, w in turned.items()}
    columns = {"bq": L0_attn_bq, "bk": L0_attn_bk, "bv": L0_attn_bv, "mu_r": L0_ffn_mu_r, "mu_k": L0_ffn_mu_k}
    arrays.update({n: np.ascontiguousarray(np.asarray(w).reshape(KH, P).T) for n, w in columns.items()})
    arrays.update(x=np.asarray(L0_attn_x), bo=np.asarray(L0_attn_bo))

    nc = bacc.Bacc("TRN2", target_bir_lowering=False, num_devices=1)
    a = {n: nc.dram_tensor(n, w.shape, mybir.dt.from_np(w.dtype), kind="ExternalInput").ap()
         for n, w in arrays.items()}
    a["out"] = nc.dram_tensor("out", (B, N, C), F32, kind="ExternalOutput").ap()
    build(nc, a)
    return run_bass_kernel_spmd(nc, [arrays], core_ids=[0]).results[0]["out"]
```

```python
from contextlib import ExitStack

import concourse.bass as bass
from concourse import mybir

F32 = mybir.dt.float32
BF16 = mybir.dt.bfloat16
I32 = mybir.dt.int32
ALU = mybir.AluOpType
ACT = mybir.ActivationFunctionType
AX = mybir.AxisListType

P = 128
B, N, C, H = 4, 2048, 256, 16
D = C // H
KH = C // P
TB = 512
TT = TB // P
BLOCKS = B * N // TB
BPB = N // TB
G = 4
UNITS = B * H // G
QB = N // TB
ITS = UNITS * QB
CH = N // P
KB = N // TB
PARTS = 3
PAIRS = ((0, 0), (1, 0), (2, 0), (0, 1), (1, 1), (0, 2))
SR = len(PAIRS) * D
MR = SR + PARTS
QRING = 4
SCALE = float(D) ** 0.5
EPS = 1e-5
RSQRT_SEED = float(0x5F3759DF)
DMA = 16


class Steps:

    CREDIT = 2

    def __init__(self, sem, names):
        self.sem, self.names = sem, names

    def start(self, eng):
        eng.sem_inc(self.sem, self.CREDIT * len(self.names))

    def done(self, ins):
        ins.then_inc(self.sem, 1)

    def done_alone(self, eng):
        eng.sem_inc(self.sem, 1)

    def value(self, block, name):
        return (block + self.CREDIT) * len(self.names) + self.names.index(name) + 1

    def wait(self, eng, block, name):
        eng.wait_ge(self.sem, self.value(block, name))


LN_STEPS = ([f"stats{t}" for t in range(TT)] + ["all stats"] + [f"meanvar{t}" for t in range(TT)] +
            ["eps", "shift", "seed"] + [f"newton{n}{s}" for n in range(3) for s in "abc"] +
            [f"norm{t}" for t in range(TT)])


def settle(eng, sem):
    eng.sem_inc(sem, 1)


def layernorm(dve, steps, blk, x, xn, stats, mv, w):
    ve, half, y, t, z = (w[:, n, :] for n in range(5))
    for n in range(TT):
        steps.done(dve.bn_stats(stats[:, n, :], x[:, n, :]))
    steps.wait(dve, blk, f"stats{TT - 1}")
    steps.done_alone(dve)
    for n in range(TT):
        steps.done(dve.bn_aggr(mv[:, n, :], stats[:, n, :]))
    steps.wait(dve, blk, f"meanvar{TT - 1}")
    steps.done(dve.tensor_scalar(ve, mv[:, :, 1], EPS, None, ALU.add))
    steps.wait(dve, blk, "eps")
    steps.done(dve.tensor_scalar(half.bitcast(I32), ve.bitcast(I32), 1, None, ALU.logical_shift_right))
    steps.wait(dve, blk, "shift")
    steps.done(dve.tensor_scalar(y.bitcast(I32), half.bitcast(I32), -1.0, RSQRT_SEED, ALU.mult, ALU.add))
    last = "seed"
    for n in range(3):
        steps.wait(dve, blk, last)
        steps.done(dve.tensor_tensor(t, y, y, ALU.mult))
        steps.wait(dve, blk, f"newton{n}a")
        steps.done(dve.scalar_tensor_tensor(out=z, in0=t, scalar=-0.5, in1=ve, op0=ALU.mult, op1=ALU.mult))
        steps.wait(dve, blk, f"newton{n}b")
        steps.done(dve.scalar_tensor_tensor(out=y, in0=z, scalar=1.5, in1=y, op0=ALU.add, op1=ALU.mult))
        last = f"newton{n}c"
    steps.wait(dve, blk, last)
    for n in range(TT):
        steps.done(dve.tensor_scalar(xn[:, n, :], x[:, n, :], mv[:, n, 0:1], y[:, n:n + 1],
                                     ALU.subtract, ALU.mult))


def make_identity(pool, ident, sem):
    pool.memset(ident[:, :], 0.0).then_inc(sem, 1)
    pool.wait_ge(sem, 1)
    pool.affine_select(out=ident[:, :], in_=ident[:, :], compare_op=ALU.not_equal, fill=1.0, base=0,
                       pattern=[[-1, P]], channel_multiplier=1).then_inc(sem, 1)


def stage_project(nc, psum, x, wqT, wkT, wvT, bq, bk, q_d, k_d, v_d):
    with ExitStack() as ctx:
        def sb(name, shape, dt):
            return ctx.enter_context(nc.sbuf_tensor(name, shape, dt))

        def sem(name):
            return ctx.enter_context(nc.semaphore(name))

        ident = sb("p_ident", [P, P], F32)
        w_sb = {n: sb(f"p_w{n}", [P, KH, C], F32) for n in "qkv"}
        bias = {n: sb(f"p_b{n}", [P, KH], F32) for n in "qk"}
        x_sb = [sb(f"p_x{s}", [P, TT, C], F32) for s in range(2)]
        xn = [sb(f"p_xn{s}", [P, TT, C], F32) for s in range(2)]
        xnT = [sb(f"p_xnT{s}", [P, KH, TB], F32) for s in range(2)]
        full = [sb(f"p_full{s}", [P, 4, TB], F32) for s in range(2)]
        rest = [sb(f"p_rest{s}", [P, 4, TB], F32) for s in range(2)]
        parts = [sb(f"p_parts{s}", [P, 4, PARTS, TB], BF16) for s in range(2)]
        v_sb = [sb(f"p_v{s}", [P, TT, C], F32) for s in range(2)]
        stats = sb("p_stats", [P, TT, 6], F32)
        mv = sb("p_mv", [P, TT, 2], F32)
        work = sb("p_work", [P, 5, TT], F32)

        s_w = sem("p_s_w")
        s_id = sem("p_s_id")
        s_gate = sem("p_s_gate")
        s_x = [sem(f"p_s_x{s}") for s in range(2)]
        s_wr = [sem(f"p_s_wr{s}") for s in range(2)]
        jobs = [("q", 0), ("q", 1), ("k", 0), ("k", 1)]
        ln = Steps(sem("p_s_ln"), LN_STEPS)
        pe = Steps(sem("p_s_pe"), [f"{n}{h}" for n, h in jobs] + ["v0", "v1"])
        pt = Steps(sem("p_s_pt"), ["turned0", "turned1"])
        act = Steps(sem("p_s_act"), ["xnT0", "xnT1"])
        av = Steps(sem("p_s_av"), [f"{s}{n}{h}" for n, h in jobs for s in ("full_", "part0_")] + ["v0", "v1"])
        spl = Steps(sem("p_s_spl"), [f"{s}{n}{h}" for n, h in jobs for s in ("rest_", "part1_", "part2_")])
        PER_SLOT = 4 + 4

        x_v = x.rearrange("b (m t p) c -> (b m) p t c", p=P, t=TT)
        block = ctx.enter_context(nc.Block())

        @block.sync
        def _(sp):
            for n, src in (("q", wqT), ("k", wkT), ("v", wvT)):
                sp.dma_start(w_sb[n][:, :, :], src.rearrange("(k p) n -> p k n", p=P)).then_inc(s_w, DMA)
            for n, src in (("q", bq), ("k", bk)):
                sp.dma_start(bias[n][:, :], src).then_inc(s_w, DMA)

            def load(s, blk, turn):
                sp.dma_start(x_sb[s][:, :, :], x_v[blk, :, :, :]).then_inc(s_x[s], DMA)

            def store(s, blk, turn):
                av.wait(sp, blk, "v1")
                settle(sp, s_gate)
                seq, tb = blk // BPB, blk % BPB
                for n in range(4):
                    sp.dma_start(v_d[seq * 4 + n, :, bass.ds(tb * TT, TT), :],
                                 v_sb[s][:, :, n * G * D:(n + 1) * G * D]).then_inc(s_wr[s], DMA)
                for j, (n, h) in enumerate(jobs):
                    spl.wait(sp, blk, f"part2_{n}{h}")
                    settle(sp, s_gate)
                    dst = (q_d[blk, h] if n == "q" else
                           k_d[seq, h, :, :, bass.ds(tb * TB, TB)])
                    sp.dma_start(dst.rearrange("a p t -> p a t"), parts[s][:, j, :, :]).then_inc(s_wr[s], DMA)

            for s in range(2):
                sp.sem_inc(s_wr[s], DMA)
                load(s, s, 0)
            with sp.Fori(0, BLOCKS // 2 - 1) as turn:
                for s in range(2):
                    blk = turn * 2 + s
                    ln.wait(sp, blk, f"norm{TT - 1}")
                    settle(sp, s_gate)
                    load(s, blk + 2, turn)
                    store(s, blk, turn)
            for s in range(2):
                store(s, BLOCKS - 2 + s, BLOCKS // 2 - 1)
            for s in range(2):
                sp.wait_ge(s_wr[s], DMA * (PER_SLOT * (BLOCKS // 2) + 1))

        @block.gpsimd
        def _(pool):
            make_identity(pool, ident, s_id)

        @block.vector
        def _(dve):
            ln.start(dve)
            spl.start(dve)
            def norm(blk, s, turn):
                dve.wait_ge(s_x[s], DMA * (turn + 1))
                layernorm(dve, ln, blk, x_sb[s], xn[s], stats, mv, work)

            def pair(turn, last):
                for s in range(2):
                    blk = turn * 2 + s
                    if not (last and s):
                        norm(blk + 1, 1 - s, turn + s)
                    for j, (n, h) in enumerate(jobs):
                        av.wait(dve, blk, f"part0_{n}{h}")
                        spl.done(dve.tensor_tensor(rest[s][:, j, :], full[s][:, j, :],
                                                   parts[s][:, j, 0, :], ALU.subtract))
                        spl.wait(dve, blk, f"rest_{n}{h}")
                        spl.done(dve.tensor_copy(parts[s][:, j, 1, :], rest[s][:, j, :]))
                        spl.wait(dve, blk, f"part1_{n}{h}")
                        spl.done(dve.tensor_tensor(parts[s][:, j, 2, :], rest[s][:, j, :],
                                                   parts[s][:, j, 1, :], ALU.subtract))

            norm(0, 0, 0)
            with dve.Fori(0, BLOCKS // 2 - 1) as turn:
                pair(turn, False)
            pair(BLOCKS // 2 - 1, True)

        @block.tensor
        def _(te):
            pe.start(te)
            pt.start(te)
            te.wait_ge(s_id, 2)
            te.wait_ge(s_w, DMA * 5)
            def turned(blk, s):
                ln.wait(te, blk, f"norm{TT - 1}")
                for h in range(KH):
                    for t in range(TT):
                        m = te.transpose(psum[:, h, t * P:(t + 1) * P], xn[s][:, t, h * P:(h + 1) * P],
                                         ident[:, :])
                    pt.done(m)

            def pair(turn, last):
                for s in range(2):
                    blk = turn * 2 + s
                    act.wait(te, blk, "xnT1")
                    av.wait(te, blk - 1, "v1")
                    for j, (n, h) in enumerate(jobs):
                        for k in range(KH):
                            m = te.matmul(psum[:, 2 + j, :], w_sb[n][:, k, h * P:(h + 1) * P],
                                          xnT[s][:, k, :], start=(k == 0), stop=(k == KH - 1))
                        pe.done(m)
                    if not (last and s):
                        turned(blk + 1, 1 - s)
                    for t in range(TT):
                        o = psum[:, 6 + t // 2, (t % 2) * C:(t % 2 + 1) * C]
                        for k in range(KH):
                            m = te.matmul(o, xnT[s][:, k, t * P:(t + 1) * P], w_sb["v"][:, k, :],
                                          start=(k == 0), stop=(k == KH - 1))
                        if t % 2:
                            pe.done(m)

            turned(0, 0)
            with te.Fori(0, BLOCKS // 2 - 1) as turn:
                pair(turn, False)
            pair(BLOCKS // 2 - 1, True)

        @block.scalar
        def _(ac):
            act.start(ac)
            av.start(ac)
            ac.wait_ge(s_w, DMA * 5)

            def keep_turned(blk, s):
                for h in range(KH):
                    pt.wait(ac, blk, f"turned{h}")
                    act.done(ac.copy(xnT[s][:, h, :], psum[:, h, :]))

            def pair(turn, last):
                for s in range(2):
                    blk = turn * 2 + s
                    ac.wait_ge(s_wr[s], DMA * (PER_SLOT * turn + 1))
                    for j, (n, h) in enumerate(jobs):
                        pe.wait(ac, blk, f"{n}{h}")
                        av.done(ac.activation(full[s][:, j, :], psum[:, 2 + j, :], ACT.Identity,
                                              bias=bias[n][:, h:h + 1]))
                        av.done(ac.activation(parts[s][:, j, 0, :], psum[:, 2 + j, :], ACT.Identity,
                                              bias=bias[n][:, h:h + 1]))
                    if not (last and s):
                        keep_turned(blk + 1, 1 - s)
                    for t in range(0, TT, 2):
                        pe.wait(ac, blk, f"v{t // 2}")
                        av.done(ac.copy(v_sb[s][:, t:t + 2, :].rearrange("p t c -> p (t c)"),
                                        psum[:, 6 + t // 2, :]))

            keep_turned(0, 0)
            with ac.Fori(0, BLOCKS // 2 - 1) as turn:
                pair(turn, False)
            pair(BLOCKS // 2 - 1, True)


def stage_attend(nc, psum, q_d, k_d, v_d, num_d, den_d):
    LEAD = CH + 4
    AHEAD = LEAD - CH
    ST, O, RING = 0, 4, 5
    NRING, TURN_AT = 3, CH - AHEAD + 1
    SLOTS = CH * KB + 2
    FIRST = LEAD * KB + 2
    with ExitStack() as ctx:
        def sb(name, shape, dt):
            return ctx.enter_context(nc.sbuf_tensor(name, shape, dt))

        def sem(name):
            return ctx.enter_context(nc.semaphore(name))

        ks = sb("a_ks", [MR, 2, G, N], BF16)
        qs = sb("a_qs", [MR, QRING, G * TB], BF16)
        v_in = sb("a_vin", [P, 2, CH, G * D], F32)
        v_st = sb("a_vst", [P, CH, G, 32], F32)
        p_sb = sb("a_p", [P, 2, G, TB], F32)
        o_sb = sb("a_o", [P, TB], F32)
        ident = sb("a_ident", [P, P], BF16)
        mx = sb("a_mx", [P, G * TT, KB], F32)
        m = sb("a_m", [P, G * TT], F32)
        m_rest = sb("a_mrest", [P, G * TT], F32)
        m_parts = sb("a_mparts", [P, PARTS, G * TT], BF16)
        m_rows = sb("a_mrows", [PARTS * G * TT, P], BF16)

        s_id = sem("a_s_id")
        s_one = sem("a_s_one")
        s_k = sem("a_s_k")
        s_q = sem("a_s_q")
        s_v = sem("a_s_v")
        s_vc = sem("a_s_vc")
        s_st = sem("a_s_st")
        s_exp = sem("a_s_exp")
        s_sp = sem("a_s_sp")
        s_mx = sem("a_s_mx")
        s_ch = sem("a_s_ch")
        s_mr = sem("a_s_mr")
        s_pv = sem("a_s_pv")
        s_oe = sem("a_s_oe")
        s_out = sem("a_s_out")
        s_te, s_sp_gate = sem("a_s_te"), sem("a_s_gate")
        K_INC, Q_INC, V_INC = DMA * len(PAIRS), DMA * len(PAIRS), DMA
        M_INC, OUT_INC = DMA * PARTS, DMA * 2 * G
        CHAIN = 5

        def stream(it, c):
            late = c >= CH - AHEAD
            return it + 1 + late, (c + AHEAD) % CH, c * KB + 2 * (c > TURN_AT)

        def slot(it, n):
            return FIRST + SLOTS * it + n, RING + (FIRST + n) % NRING

        TURN = (TURN_AT + 1) * KB
        SKIPPED = TURN - (CH - AHEAD) * KB
        BEFORE = range(-AHEAD, CH)

        block = ctx.enter_context(nc.Block())

        @block.sync
        def _(sp):
            def load_k(piece):
                dst = ks[:, (piece // G) % 2, piece % G, :]
                for r, (_, a) in enumerate(PAIRS):
                    sp.dma_start(dst[r * D:(r + 1) * D, :],
                                 k_d[piece // H, (piece // (H // KH)) % KH, a,
                                     bass.ds((piece % (H // KH)) * D, D), :]).then_inc(s_k, DMA)

            def load_q(it):
                seq, grp, qb = it // (G * QB), (it // QB) % G, it % QB
                src = q_d[seq * QB + qb, grp // 2, :, bass.ds((grp % 2) * G * D, G * D), :].rearrange(
                    "a (g d) t -> a d g t", d=D)
                for r, (a, _) in enumerate(PAIRS):
                    sp.dma_start(qs[r * D:(r + 1) * D, it % QRING, :].rearrange("p (g t) -> p g t", g=G),
                                 src[a]).then_inc(s_q, DMA)

            def load_v(piece):
                c = (piece % G) * (CH // G)
                sp.dma_start(v_in[:, (piece // G) % 2, bass.ds(c, CH // G), :],
                             v_d[piece // G, :, bass.ds(c, CH // G), :]).then_inc(s_v, DMA)

            def rows(it):
                sp.wait_ge(s_mx, NRING + slot(it - 1, TURN)[0] + 2)
                settle(sp, s_sp_gate)
                for a in range(PARTS):
                    sp.dma_start(qs[SR + a:SR + a + 1, it % QRING, :].rearrange("o (n p) -> o n p", p=P),
                                 m_rows[a * G * TT:(a + 1) * G * TT, :]).then_inc(s_mr, DMA)

            def out(it):
                sp.wait_ge(s_oe, it + 2)
                settle(sp, s_sp_gate)
                seq, grp, qb = it // (G * QB), (it // QB) % G, it % QB
                for g in range(G):
                    for dst, row, n, w in ((num_d, 32 * g, D, D), (den_d, 32 * g + D, 1, 1)):
                        sp.dma_start(dst[bass.ds((grp * G + g) * w, n), bass.ds(seq * N + qb * TB, TB)],
                                     o_sb[row:row + n, :]).then_inc(s_out, DMA)

            def body(it, k, q):
                sp.wait_ge(s_st, it * 2 * CH + 1)
                sp.wait_ge(s_vc, it * CH + CH)
                settle(sp, s_sp_gate)
                if k:
                    load_k(it + G)
                    load_v(it + G)
                else:
                    sp.sem_inc(s_k, K_INC)
                    sp.sem_inc(s_v, V_INC)
                if q:
                    load_q(it + QRING - 1)
                else:
                    sp.sem_inc(s_q, Q_INC)
                if not isinstance(it, int) or it + 1 < ITS:
                    rows(it + 1)
                sp.wait_ge(s_k, K_INC * (it + G + 1))
                settle(sp, s_sp_gate)
                sp.wait_ge(s_v, V_INC * (it + G + 1))
                settle(sp, s_sp_gate)
                sp.wait_ge(s_q, Q_INC * (it + QRING))
                settle(sp, s_sp_gate)
                out(it)

            sp.sem_inc(s_out, DMA)
            sp.sem_inc(s_mr, DMA)
            for n in range(G):
                load_k(n)
                if n < QRING - 1:
                    load_q(n)
                load_v(n)
                sp.wait_ge(s_k, K_INC * (n + 1))
                sp.wait_ge(s_q, Q_INC * min(n + 1, QRING - 1))
            rows(0)
            with sp.Fori(0, ITS - G) as it:
                body(it, True, True)
            for it in range(ITS - G, ITS):
                body(it, False, it + QRING - 1 < ITS)
            sp.wait_ge(s_out, DMA + OUT_INC * ITS)

        @block.gpsimd
        def _(pool):
            make_identity(pool, ident, s_id)
            pool.wait_ge(s_id, 2)
            pool.memset(v_st[:, :, :, :], 0.0).then_inc(s_one, 1)
            pool.wait_ge(s_one, 1)
            pool.memset(v_st[:, :, :, D:D + 1], 1.0).then_inc(s_one, 1)
            for u in range(2):
                pool.wait_ge(s_one, 2 + u)
                pool.memset(ks[SR:MR, u, :, :], 1.0).then_inc(s_one, 1)
            pool.wait_ge(s_one, 4)

            def copy_v(it, c):
                pool.tensor_copy(v_st[:, c, :, 0:D],
                                 v_in[:, (it // QB) % 2, c, :].rearrange("p (g d) -> p g d", g=G)
                                 ).then_inc(s_vc, 1)

            pool.wait_ge(s_v, V_INC * G)
            for c in range(CH):
                copy_v(0, c)
            with pool.Fori(0, ITS - 1) as it:
                for c in range(CH):
                    if c in (0, CH - CH // G):
                        pool.wait_ge(s_v, V_INC * (it + G + (c > 0)))
                    pool.wait_ge(s_pv, it * CH + c + 3)
                    copy_v(it + 1, c)

        @block.scalar
        def _(ac):
            ac.sem_inc(s_exp, 2)
            ac.sem_inc(s_oe, 1)
            with ac.Fori(0, ITS) as it:
                for c in range(CH):
                    ac.wait_ge(s_pv, it * CH + c + 1)
                    for half in range(2):
                        ac.wait_ge(s_st, it * 2 * CH + 2 * c + half + 1)
                        ac.activation(p_sb[:, c % 2, 2 * half:2 * half + 2, :],
                                      psum[:, ST + 2 * half:ST + 2 * half + 2, :], ACT.Exp,
                                      scale=SCALE).then_inc(s_exp, 1)
                ac.wait_ge(s_pv, it * CH + CH + 2)
                ac.wait_ge(s_out, it * OUT_INC + DMA)
                ac.copy(o_sb[:, :], psum[:, O, :]).then_inc(s_oe, 1)

        @block.vector
        def _(dve):
            def reduce(it, pair, first):
                for kb in range(KB):
                    n, bank = slot(it, first + kb)
                    dve.wait_ge(s_sp, n + 1)
                    dve.tensor_reduce(mx[:, pair, kb:kb + 1], psum[:, bank, :], AX.X, ALU.max
                                      ).then_inc(s_mx, 1)

            def chain(it, blk, first):
                dve.wait_ge(s_mx, NRING + slot(it, first + KB)[0])
                dve.tensor_reduce(m[:, :], mx[:, :, :], AX.X, ALU.max).then_inc(s_ch, 1)
                dve.wait_ge(s_ch, blk * CHAIN + 1)
                dve.tensor_scalar(m_parts[:, 0, :], m[:, :], -1.0, None, ALU.mult).then_inc(s_ch, 1)
                dve.wait_ge(s_ch, blk * CHAIN + 2)
                dve.scalar_tensor_tensor(out=m_rest[:, :], in0=m[:, :], scalar=-1.0, in1=m_parts[:, 0, :],
                                         op0=ALU.mult, op1=ALU.subtract).then_inc(s_ch, 1)
                dve.wait_ge(s_ch, blk * CHAIN + 3)
                dve.tensor_copy(m_parts[:, 1, :], m_rest[:, :]).then_inc(s_ch, 1)
                dve.wait_ge(s_ch, blk * CHAIN + 4)
                dve.tensor_tensor(m_parts[:, 2, :], m_rest[:, :], m_parts[:, 1, :], ALU.subtract
                                  ).then_inc(s_ch, 1)

            def keep_rows(it):
                n, bank = slot(it, TURN)
                dve.wait_ge(s_sp, n + 2)
                dve.wait_ge(s_mr, M_INC * (it + 1) + DMA)
                dve.tensor_copy(m_rows[:, :], psum[0:PARTS * G * TT, bank, 0:P // 2].bitcast(BF16)
                                ).then_inc(s_mx, 2)

            def body(it, steps):
                for c in steps:
                    blk, pair, first = stream(it, c)
                    reduce(it, pair, first)
                    if pair == CH - 1:
                        chain(it, blk, first)
                    if c == TURN_AT:
                        keep_rows(it)

            body(-1, BEFORE)
            with dve.Fori(0, ITS - 2) as it:
                body(it, range(CH))
            body(ITS - 2, range(CH - AHEAD))
            dve.wait_ge(s_sp, slot(ITS - 2, TURN)[0])
            dve.sem_inc(s_mx, SKIPPED)
            keep_rows(ITS - 2)

        @block.tensor
        def _(te):
            def scores(it, c, half):
                te.wait_ge(s_exp, it * 2 * CH + 2 * c + half + 1)
                for g in range(2 * half, 2 * half + 2):
                    mm = te.matmul(psum[:, ST + g, :], ks[0:MR, (it // QB) % 2, g, c * P:(c + 1) * P],
                                   qs[0:MR, it % QRING, g * TB:(g + 1) * TB], start=True, stop=True)
                mm.then_inc(s_st, 1)

            def peak(it, c, kbs):
                blk, pair, first = stream(it, c)
                for kb in kbs:
                    n, bank = slot(it, first + kb)
                    te.wait_ge(s_mx, n + 1)
                    te.matmul(psum[:, bank, :], qs[0:SR, blk % QRING, pair * P:(pair + 1) * P],
                              ks[0:SR, (blk // QB) % 2, pair // TT, kb * TB:(kb + 1) * TB],
                              start=True, stop=True).then_inc(s_sp, 1)

            def turn(it):
                n, bank = slot(it, TURN)
                te.wait_ge(s_ch, CHAIN * (it + 2))
                te.wait_ge(s_mx, n + 1)
                settle(te, s_te)
                te.transpose(psum[0:PARTS * G * TT, bank, 0:P // 2].bitcast(BF16),
                             m_parts[:, :, :].rearrange("p a n -> p (a n)"), ident[:, :]).then_inc(s_sp, 2)

            def times_v(it, c):
                te.wait_ge(s_exp, it * 2 * CH + 2 * c + 4)
                te.wait_ge(s_vc, it * CH + c + 1)
                if c == 0:
                    te.wait_ge(s_oe, it + 1)
                for g in range(G):
                    mm = te.matmul(psum[32 * g:32 * g + 32, O, :], v_st[:, c, g, :],
                                   p_sb[:, c % 2, g, :], start=(c == 0), stop=(c == CH - 1))
                mm.then_inc(s_pv, 1)

            def body(it, steps):
                te.wait_ge(s_mr, M_INC * (it + 1) + DMA)
                for c in range(CH):
                    blk, pair, _ = stream(it, c)
                    ahead = c < steps
                    if ahead and c == 0:
                        te.wait_ge(s_k, K_INC * (it + G))
                    if ahead and pair == 3 * TT:
                        te.wait_ge(s_k, K_INC * (it + G + 1))
                    if ahead and pair == 0:
                        te.wait_ge(s_q, Q_INC * (it + 3))
                    scores(it, c, 0)
                    if ahead:
                        peak(it, c, (0,))
                    scores(it, c, 1)
                    if ahead:
                        peak(it, c, (1,))
                    if c:
                        times_v(it, c - 1)
                    if ahead:
                        peak(it, c, (2, 3))
                    if c == steps and steps:
                        te.wait_ge(s_mx, NRING + slot(it, TURN)[0] - SKIPPED)
                        te.sem_inc(s_sp, SKIPPED)
                    if c == TURN_AT and steps:
                        turn(it)
                times_v(it, CH - 1)

            te.sem_inc(s_pv, 2)
            te.sem_inc(s_mx, NRING)
            te.wait_ge(s_id, 2)
            te.wait_ge(s_q, Q_INC)
            for n in range(G):
                te.wait_ge(s_k, K_INC * (n + 1))
                for pair in range(TT * n, TT * n + TT):
                    peak(-1, pair - AHEAD, range(KB))
            te.wait_ge(s_one, 4)
            te.wait_ge(s_q, Q_INC * (QRING - 1))
            for c in range(CH - AHEAD, CH):
                peak(-1, c, range(KB))
                if c == TURN_AT:
                    turn(-1)
            with te.Fori(0, ITS - 2) as it:
                body(it, CH)
            body(ITS - 2, CH - AHEAD)
            body(ITS - 1, 0)


def stage_mix(nc, psum, x, num_d, den_d, rden_d, bv, woT, bo, wrT, wkT, wvT, mu_r, mu_k, out):
    with ExitStack() as ctx:
        def sb(name, shape, dt):
            return ctx.enter_context(nc.sbuf_tensor(name, shape, dt))

        def sem(name):
            return ctx.enter_context(nc.semaphore(name))

        def two(name, shape):
            return [sb(f"m_{name}{s}", shape, F32) for s in range(2)]

        ident = sb("m_ident", [P, P], F32)
        w_sb = {n: sb(f"m_w{n}", [P, KH, C], F32) for n in "orkv"}
        col = {n: sb(f"m_{n}", [P, KH], F32) for n in ("bv", "mr", "mk")}
        bo_sb = sb("m_bo", [P, C], F32)
        x_sb, x1 = two("x", [P, TT, C]), two("x1", [P, TT, C])
        num, rden, hT = two("num", [P, KH, TB]), two("rden", [P, KH, TB]), two("hT", [P, KH, TB])
        xn = sb("m_xn", [P, TT, C], F32)
        xT = two("xT", [P, KH, TB + 1])
        diff = sb("m_diff", [P, KH, TB], F32)
        xr, xk = two("xr", [P, KH, TB]), two("xk", [P, KH, TB])
        kr, ka = sb("m_kr", [P, KH, TB], F32), sb("m_ka", [P, KH, TB], F32)
        gate = two("gate", [P, TT, C])
        y = two("y", [P, TT, C])
        W = H * B * N // P
        den, inv = sb("m_den", [P, W], F32), sb("m_inv", [P, W], F32)
        stats = sb("m_stats", [P, TT, 6], F32)
        mv = sb("m_mv", [P, TT, 2], F32)
        work = sb("m_work", [P, 5, TT], F32)

        s_w, s_id, s_gate = sem("m_s_w"), sem("m_s_id"), sem("m_s_gate")
        s_den, s_inv, s_rden = sem("m_s_den"), sem("m_s_inv"), sem("m_s_rden")
        s_in = [sem(f"m_s_in{s}") for s in range(2)]
        s_out = [sem(f"m_s_out{s}") for s in range(2)]
        HH = H // KH
        N_IN = (HH + 2) * KH
        ln = Steps(sem("m_s_ln"), ["x1"] + LN_STEPS)
        pf = Steps(sem("m_s_pf"), ["proj"])
        pf_t = Steps(sem("m_s_pt"), ["turned0", "turned1"])
        pb_ = Steps(sem("m_s_pb"), ["k", "r", "v"])
        gf = Steps(sem("m_s_gf"), ["h0", "h1", "xb"])
        gb = Steps(sem("m_s_gb"), ["sq", "y"])
        af = Steps(sem("m_s_af"), ["bias0", "bias1"])
        at = Steps(sem("m_s_at"), ["xT0", "xT1"])
        ab = Steps(sem("m_s_ab"), ["relu", "gate"])
        vb = Steps(sem("m_s_vb"), ["prev", "diff", "xk0", "xk1", "xr0", "xr1"])
        vy = Steps(sem("m_s_vy"), ["gated"])
        NW = 4 + 3 + 1

        x_v = x.rearrange("b (m t p) c -> (b m) p t c", p=P, t=TT)
        out_v = out.rearrange("b (m t p) c -> (b m) p t c", p=P, t=TT)
        block = ctx.enter_context(nc.Block())

        def turns(eng, turn):
            with eng.Fori(0, B - 1) as seq:
                for n in range(BPB):
                    turn(seq * BPB + n, n)
            for n in range(BPB):
                turn((B - 1) * BPB + n, n)

        def there(blk):
            return not isinstance(blk, int) or blk < BLOCKS

        def uses(blk):
            return blk // 2

        @block.sync
        def _(sp):
            flat = "h (a w) -> (h a) w"
            sp.dma_start(den[:, :], den_d.rearrange(flat, w=W)).then_inc(s_den, DMA)
            for n, src in (("o", woT), ("r", wrT), ("k", wkT), ("v", wvT)):
                sp.dma_start(w_sb[n][:, :, :], src.rearrange("(k p) n -> p k n", p=P)).then_inc(s_w, DMA)
            for n, src in (("bv", bv), ("mr", mu_r), ("mk", mu_k)):
                sp.dma_start(col[n][:, :], src).then_inc(s_w, DMA)
            sp.dma_start(bo_sb[:, :], bo.rearrange("(o c) -> o c", o=1).to_broadcast([P, C])
                         ).then_inc(s_w, DMA)

            def front(blk, n):
                s = n % 2
                gf.wait(sp, blk - 2, "xb")
                ln.wait(sp, blk - 2, "x1")
                settle(sp, s_gate)
                tok = bass.ds(blk * TB, TB)
                for k in range(KH):
                    sp.dma_start(num[s][:, k, :], num_d[k * P:(k + 1) * P, tok]).then_inc(s_in[s], DMA)
                    for h in range(HH):
                        sp.dma_start(rden[s][h * D:(h + 1) * D, k, :],
                                     rden_d[k * HH + h:k * HH + h + 1, tok].to_broadcast([D, TB])
                                     ).then_inc(s_in[s], DMA)
                    sp.dma_start(x_sb[s][:, 2 * k:2 * k + 2, :], x_v[blk, :, 2 * k:2 * k + 2, :]
                                 ).then_inc(s_in[s], DMA)

            def back(blk, n):
                gb.wait(sp, blk, "y")
                settle(sp, s_gate)
                sp.dma_start(out_v[blk, :, :, :], y[n % 2][:, :, :]).then_inc(s_out[n % 2], DMA)

            for s in range(2):
                sp.sem_inc(s_out[s], DMA)
            def turn(blk, n):
                if there(blk + 3):
                    front(blk + 3, n + 3)
                back(blk, n)

            sp.wait_ge(s_inv, 1)
            sp.dma_start(rden_d.rearrange(flat, w=W), inv[:, :]).then_inc(s_rden, DMA)
            sp.wait_ge(s_rden, DMA)
            for n in range(3):
                front(n, n)
            turns(sp, turn)
            for s in range(2):
                sp.wait_ge(s_out[s], DMA * (BLOCKS // 2 + 1))

        @block.gpsimd
        def _(pool):
            gf.start(pool)
            gb.start(pool)
            make_identity(pool, ident, s_id)
            pool.wait_ge(s_w, DMA * NW)

            def front(blk, n):
                s = n % 2
                pool.wait_ge(s_in[s], DMA * N_IN * (uses(blk) + 1))
                for k in range(KH):
                    pf.wait(pool, blk - 2, "proj")
                    gf.done(pool.tensor_tensor(hT[s][:, k, :], num[s][:, k, :], rden[s][:, k, :], ALU.mult))
                gf.done(pool.tensor_tensor(x_sb[s][:, :, :], x_sb[s][:, :, :],
                                           bo_sb[:, :].unsqueeze(1).to_broadcast([P, TT, C]), ALU.add))

            def turn(blk, n):
                s = n % 2
                ab.wait(pool, blk, "relu")
                pb_.wait(pool, blk - 1, "v")
                gb.done(pool.tensor_tensor(ka[:, :, :], kr[:, :, :], kr[:, :, :], ALU.mult))
                if there(blk + 2):
                    front(blk + 2, n + 2)
                vy.wait(pool, blk, "gated")
                gb.done(pool.tensor_tensor(y[s][:, :, :], y[s][:, :, :], x1[s][:, :, :], ALU.add))

            for n in range(2):
                front(n, n)
            turns(pool, turn)

        @block.scalar
        def _(ac):
            for steps in (af, at, ab):
                steps.start(ac)
            ac.wait_ge(s_w, DMA * NW)

            def add_bias(blk, n):
                for k in range(KH):
                    gf.wait(ac, blk, f"h{k}")
                    af.done(ac.activation(hT[n % 2][:, k, :], hT[n % 2][:, k, :], ACT.Identity,
                                          bias=col["bv"][:, k:k + 1]))

            def keep_turned(blk, n):
                for k in range(KH):
                    pf_t.wait(ac, blk, f"turned{k}")
                    vb.wait(ac, blk - 1, "prev")
                    at.done(ac.copy(xT[n % 2][:, k, 1:TB + 1], psum[:, 2 + k, :]))

            def turn(blk, n):
                s = n % 2
                pb_.wait(ac, blk, "k")
                gb.wait(ac, blk - 1, "sq")
                ab.done(ac.activation(kr[:, :, :], psum[:, 4:6, :], ACT.Relu))
                pb_.wait(ac, blk, "r")
                vy.wait(ac, blk - 2, "gated")
                ab.done(ac.activation(gate[s][:, :, :].rearrange("p t c -> p (t c)"),
                                      psum[:, 6:8, :].rearrange("p a c -> p (a c)"), ACT.Sigmoid))
                if there(blk + 1):
                    keep_turned(blk + 1, n + 1)
                if there(blk + 2):
                    add_bias(blk + 2, n + 2)

            add_bias(0, 0)
            keep_turned(0, 0)
            add_bias(1, 1)
            turns(ac, turn)

        @block.vector
        def _(dve):
            for steps in (ln, vb, vy):
                steps.start(dve)
            dve.wait_ge(s_den, DMA)
            dve.reciprocal(inv[:, :], den[:, :]).then_inc(s_inv, 1)
            dve.wait_ge(s_w, DMA * NW)

            def front(blk, n):
                s = n % 2
                pf.wait(dve, blk, "proj")
                gf.wait(dve, blk, "xb")
                gb.wait(dve, blk - 2, "y")
                ln.done(dve.tensor_tensor(x1[s][:, :, :].rearrange("p t c -> p (t c)"),
                                          psum[:, 0:2, :].rearrange("p a c -> p (a c)"),
                                          x_sb[s][:, :, :].rearrange("p t c -> p (t c)"), ALU.add))
                ln.wait(dve, blk, "x1")
                pf_t.wait(dve, blk - 1, "turned1")
                layernorm(dve, ln, blk, x1[s], xn, stats, mv, work)
                at.wait(dve, blk, "xT1")
                if n % BPB == 0:
                    vb.done(dve.memset(xT[s][:, :, 0:1], 0.0))
                else:
                    vb.done(dve.tensor_copy(xT[s][:, :, 0:1], xT[1 - s][:, :, TB:TB + 1]))
                vb.wait(dve, blk, "prev")
                vb.done(dve.tensor_tensor(diff[:, :, :], xT[s][:, :, 1:TB + 1], xT[s][:, :, 0:TB],
                                          ALU.subtract))
                vb.wait(dve, blk, "diff")
                pb_.wait(dve, blk - 2, "r")
                for name, dst, mu in (("xk", xk, "mk"), ("xr", xr, "mr")):
                    for k in range(KH):
                        vb.done(dve.scalar_tensor_tensor(out=dst[s][:, k, :], in0=diff[:, k, :],
                                                         scalar=col[mu][:, k:k + 1], in1=xT[s][:, k, 0:TB],
                                                         op0=ALU.mult, op1=ALU.add))

            def back(blk, n):
                s = n % 2
                pb_.wait(dve, blk, "v")
                ab.wait(dve, blk, "gate")
                dve.wait_ge(s_out[s], DMA * (uses(blk) + 1))
                vy.done(dve.tensor_tensor(y[s][:, :, :].rearrange("p t c -> p (t c)"),
                                          psum[:, 4:6, :].rearrange("p a c -> p (a c)"),
                                          gate[s][:, :, :].rearrange("p t c -> p (t c)"), ALU.mult))

            def turn(blk, n):
                if there(blk + 1):
                    front(blk + 1, n + 1)
                back(blk, n)

            front(0, 0)
            turns(dve, turn)

        @block.tensor
        def _(te):
            for steps in (pf, pf_t, pb_):
                steps.start(te)
            te.wait_ge(s_w, DMA * NW)
            te.wait_ge(s_id, 2)

            def by_token(bank, lhsT, w, steps):
                for t in range(TT):
                    for k in range(KH):
                        mm = te.matmul(psum[:, bank + t // 2, (t % 2) * C:(t % 2 + 1) * C],
                                       lhsT[:, k, t * P:(t + 1) * P], w[:, k, :],
                                       start=(k == 0), stop=(k == KH - 1))
                steps.done(mm)

            def proj(blk, n):
                af.wait(te, blk, "bias1")
                ln.wait(te, blk - 1, "x1")
                by_token(0, hT[n % 2], w_sb["o"], pf)

            def turned(blk, n):
                ln.wait(te, blk, f"norm{TT - 1}")
                at.wait(te, blk - 1, "xT1")
                for h in range(KH):
                    for t in range(TT):
                        mm = te.transpose(psum[:, 2 + h, t * P:(t + 1) * P], xn[:, t, h * P:(h + 1) * P],
                                          ident[:, :])
                    pf_t.done(mm)

            def products(blk, n):
                s = n % 2
                vb.wait(te, blk, "xk1")
                vy.wait(te, blk - 1, "gated")
                for h in range(KH):
                    for k in range(KH):
                        mm = te.matmul(psum[:, 4 + h, :], w_sb["k"][:, k, h * P:(h + 1) * P], xk[s][:, k, :],
                                       start=(k == 0), stop=(k == KH - 1))
                pb_.done(mm)
                vb.wait(te, blk, "xr1")
                ab.wait(te, blk - 1, "gate")
                by_token(6, xr[s], w_sb["r"], pb_)

            def value(blk, n):
                gb.wait(te, blk, "sq")
                by_token(4, ka, w_sb["v"], pb_)

            def turn(blk, n):
                if there(blk + 1):
                    proj(blk + 1, n + 1)
                products(blk, n)
                if there(blk + 1):
                    turned(blk + 1, n + 1)
                value(blk, n)

            proj(0, 0)
            turned(0, 0)
            turns(te, turn)


def build(nc, a):
    dram = nc.dram_tensor
    q_d = dram("q_parts", (BLOCKS, KH, PARTS, P, TB), BF16).ap()
    k_d = dram("k_parts", (B, KH, PARTS, P, N), BF16).ap()
    v_d = dram("v_rows", (UNITS, P, CH, G * D), F32).ap()
    num_d = dram("numerators", (C, B * N), F32).ap()
    den_d = dram("denominators", (H, B * N), F32).ap()
    rden_d = dram("inverse_denominators", (H, B * N), F32).ap()
    with nc.psum_tensor("psum", [P, 8, TB], F32) as psum:
        stage_project(nc, psum, a["x"], a["wqT"], a["wkT"], a["wvT"], a["bq"], a["bk"], q_d, k_d, v_d)
        stage_attend(nc, psum, q_d, k_d, v_d, num_d, den_d)
        stage_mix(nc, psum, a["x"], num_d, den_d, rden_d, a["bv"], a["woT"], a["bo"], a["fwrT"], a["fwkT"],
                  a["fwvT"], a["mu_r"], a["mu_k"], a["out"])


def kernel(L0_attn_x, L0_attn_Wq, L0_attn_bq, L0_attn_Wk, L0_attn_bk, L0_attn_Wv, L0_attn_bv,
           L0_attn_Wo, L0_attn_bo, L0_ffn_W_r, L0_ffn_W_k, L0_ffn_W_v, L0_ffn_mu_r, L0_ffn_mu_k):
    import concourse.bacc as bacc
    import numpy as np
    from concourse.bass_utils import run_bass_kernel_spmd

    turned = {"wqT": L0_attn_Wq, "wkT": L0_attn_Wk, "wvT": L0_attn_Wv, "woT": L0_attn_Wo,
              "fwrT": L0_ffn_W_r, "fwkT": L0_ffn_W_k, "fwvT": L0_ffn_W_v}
    arrays = {n: np.ascontiguousarray(np.asarray(w).T) for n, w in turned.items()}
    columns = {"bq": L0_attn_bq, "bk": L0_attn_bk, "bv": L0_attn_bv, "mu_r": L0_ffn_mu_r, "mu_k": L0_ffn_mu_k}
    arrays.update({n: np.ascontiguousarray(np.asarray(w).reshape(KH, P).T) for n, w in columns.items()})
    arrays.update(x=np.asarray(L0_attn_x), bo=np.asarray(L0_attn_bo))

    nc = bacc.Bacc("TRN2", target_bir_lowering=False, num_devices=1)
    a = {n: nc.dram_tensor(n, w.shape, mybir.dt.from_np(w.dtype), kind="ExternalInput").ap()
         for n, w in arrays.items()}
    a["out"] = nc.dram_tensor("out", (B, N, C), F32, kind="ExternalOutput").ap()
    build(nc, a)
    return run_bass_kernel_spmd(nc, [arrays], core_ids=[0]).results[0]["out"]
```

```python
from contextlib import ExitStack

import concourse.bass as bass
from concourse import mybir

F32 = mybir.dt.float32
BF16 = mybir.dt.bfloat16
I32 = mybir.dt.int32
ALU = mybir.AluOpType
ACT = mybir.ActivationFunctionType
AX = mybir.AxisListType

P = 128
B, N, C, H = 4, 2048, 256, 16
D = C // H
KH = C // P
TB = 512
TT = TB // P
BLOCKS = B * N // TB
BPB = N // TB
G = 4
UNITS = B * H // G
QB = N // TB
ITS = UNITS * QB
CH = N // P
KB = N // TB
PARTS = 3
PAIRS = ((0, 0), (1, 0), (2, 0), (0, 1), (1, 1), (0, 2))
SR = len(PAIRS) * D
MR = SR + PARTS
QRING = 4
OUTPUTS = 2 * G
STORES = 4 + 4
SCALE = float(D) ** 0.5
EPS = 1e-5
RSQRT_SEED = float(0x5F3759DF)
DMA = 16


class Steps:

    CREDIT = 2

    def __init__(self, sem, names):
        self.sem, self.names = sem, names

    def start(self, eng):
        eng.sem_inc(self.sem, self.CREDIT * len(self.names))

    def done(self, ins):
        ins.then_inc(self.sem, 1)

    def done_alone(self, eng):
        eng.sem_inc(self.sem, 1)

    def value(self, block, name):
        return (block + self.CREDIT) * len(self.names) + self.names.index(name) + 1

    def wait(self, eng, block, name):
        eng.wait_ge(self.sem, self.value(block, name))


LN_STEPS = ([f"stats{t}" for t in range(TT)] + ["all stats"] + [f"meanvar{t}" for t in range(TT)] +
            ["eps", "shift", "seed"] + [f"newton{n}{s}" for n in range(3) for s in "abc"] +
            [f"norm{t}" for t in range(TT)])


def settle(eng, sem):
    eng.sem_inc(sem, 1)


def layernorm(dve, steps, blk, x, xn, stats, mv, w, ready=None):
    ve, half, y, t, z = (w[:, n, :] for n in range(5))
    for n in range(TT):
        if ready:
            steps.wait(dve, blk, ready[n])
        steps.done(dve.bn_stats(stats[:, n, :], x[:, n, :]))
    steps.wait(dve, blk, f"stats{TT - 1}")
    steps.done_alone(dve)
    for n in range(TT):
        steps.done(dve.bn_aggr(mv[:, n, :], stats[:, n, :]))
    steps.wait(dve, blk, f"meanvar{TT - 1}")
    steps.done(dve.tensor_scalar(ve, mv[:, :, 1], EPS, None, ALU.add))
    steps.wait(dve, blk, "eps")
    steps.done(dve.tensor_scalar(half.bitcast(I32), ve.bitcast(I32), 1, None, ALU.logical_shift_right))
    steps.wait(dve, blk, "shift")
    steps.done(dve.tensor_scalar(y.bitcast(I32), half.bitcast(I32), -1.0, RSQRT_SEED, ALU.mult, ALU.add))
    last = "seed"
    for n in range(3):
        steps.wait(dve, blk, last)
        steps.done(dve.tensor_tensor(t, y, y, ALU.mult))
        steps.wait(dve, blk, f"newton{n}a")
        steps.done(dve.scalar_tensor_tensor(out=z, in0=t, scalar=-0.5, in1=ve, op0=ALU.mult, op1=ALU.mult))
        steps.wait(dve, blk, f"newton{n}b")
        steps.done(dve.scalar_tensor_tensor(out=y, in0=z, scalar=1.5, in1=y, op0=ALU.add, op1=ALU.mult))
        last = f"newton{n}c"
    steps.wait(dve, blk, last)
    for n in range(TT):
        steps.done(dve.tensor_scalar(xn[:, n, :], x[:, n, :], mv[:, n, 0:1], y[:, n:n + 1],
                                     ALU.subtract, ALU.mult))


def make_identity(pool, ident, sem):
    pool.memset(ident[:, :], 0.0).then_inc(sem, 1)
    pool.wait_ge(sem, 1)
    pool.affine_select(out=ident[:, :], in_=ident[:, :], compare_op=ALU.not_equal, fill=1.0, base=0,
                       pattern=[[-1, P]], channel_multiplier=1).then_inc(sem, 1)


class AttendInputs:
    K_INC, Q_INC, V_INC = DMA * len(PAIRS), DMA * len(PAIRS), DMA

    def __init__(self, ctx, nc, q_d, k_d, v_d):
        self.q_d, self.k_d, self.v_d = q_d, k_d, v_d
        self.ks = ctx.enter_context(nc.sbuf_tensor("a_ks", [MR, 2, G, N], BF16))
        self.qs = ctx.enter_context(nc.sbuf_tensor("a_qs", [MR, QRING, G * TB], BF16))
        self.v_in = ctx.enter_context(nc.sbuf_tensor("a_vin", [P, 2, CH, G * D], F32))
        self.s_k = ctx.enter_context(nc.semaphore("a_s_k"))
        self.s_q = ctx.enter_context(nc.semaphore("a_s_q"))
        self.s_v = ctx.enter_context(nc.semaphore("a_s_v"))
        self.s_wr = [ctx.enter_context(nc.semaphore(f"p_s_wr{s}")) for s in range(2)]

    def load_k(self, sp, piece):
        dst = self.ks[:, (piece // G) % 2, piece % G, :]
        for r, (_, a) in enumerate(PAIRS):
            sp.dma_start(dst[r * D:(r + 1) * D, :],
                         self.k_d[piece // H, (piece // (H // KH)) % KH, a,
                                  bass.ds((piece % (H // KH)) * D, D), :]).then_inc(self.s_k, DMA)

    def load_q(self, sp, it):
        seq, grp, qb = it // (G * QB), (it // QB) % G, it % QB
        src = self.q_d[seq * QB + qb, grp // 2, :, bass.ds((grp % 2) * G * D, G * D), :].rearrange(
            "a (g d) t -> a d g t", d=D)
        for r, (a, _) in enumerate(PAIRS):
            sp.dma_start(self.qs[r * D:(r + 1) * D, it % QRING, :].rearrange("p (g t) -> p g t", g=G),
                         src[a]).then_inc(self.s_q, DMA)

    def load_v(self, sp, piece):
        c = (piece % G) * (CH // G)
        sp.dma_start(self.v_in[:, (piece // G) % 2, bass.ds(c, CH // G), :],
                     self.v_d[piece // G, :, bass.ds(c, CH // G), :]).then_inc(self.s_v, DMA)

    def first(self, sp, n):
        sp.wait_ge(self.s_k, self.K_INC * n)
        sp.wait_ge(self.s_q, self.Q_INC * min(n, QRING - 1))
        sp.wait_ge(self.s_v, self.V_INC * n)
        self.load_k(sp, n)
        if n < QRING - 1:
            self.load_q(sp, n)
        self.load_v(sp, n)


class MixInputs:
    HH = H // KH
    N_IN = (HH + 2) * KH
    W = H * N // P
    NW = 4 + 3 + 1

    def __init__(self, ctx, nc, x, num_d, den_d, rden_d, bv, woT, bo, wrT, wkT, wvT, mu_r, mu_k):
        def sb(name, shape):
            return ctx.enter_context(nc.sbuf_tensor(name, shape, F32))

        def sem(name):
            return ctx.enter_context(nc.semaphore(name))

        def two(name, shape):
            return [sb(f"m_{name}{s}", shape) for s in range(2)]

        self.x_v = x.rearrange("b (m t p) c -> (b m) p t c", p=P, t=TT)
        self.num_d, self.den_d, self.rden_d = num_d, den_d, rden_d
        self.weights = {"o": woT, "r": wrT, "k": wkT, "v": wvT}
        self.columns = {"bv": bv, "mr": mu_r, "mk": mu_k}
        self.bo = bo
        self.w_sb = {n: sb(f"m_w{n}", [P, KH, C]) for n in "orkv"}
        self.col = {n: sb(f"m_{n}", [P, KH]) for n in ("bv", "mr", "mk")}
        self.bo_sb = sb("m_bo", [P, C])
        self.x_sb = two("x", [P, TT, C])
        self.num, self.rden, self.hT = (two(n, [P, KH, TB]) for n in ("num", "rden", "hT"))
        self.den, self.inv = sb("m_den", [P, B, self.W]), sb("m_inv", [P, B, self.W])
        self.o_sb = sb("a_o", [P, TB])
        self.s_w, self.s_gate, self.s_inv = sem("m_s_w"), sem("m_s_gate"), sem("m_s_inv")
        self.s_den, self.s_rden = ([sem(f"m_s_{n}{seq}") for seq in range(B)] for n in ("den", "rden"))
        self.s_in = [sem(f"m_s_in{s}") for s in range(2)]
        self.s_num = sem("a_s_out")
        self.ln = Steps(sem("m_s_ln"), ["x10", "x11"] + LN_STEPS)
        self.pf = Steps(sem("m_s_pf"), ["proj0", "proj"])
        self.gf = Steps(sem("m_s_gf"), ["h0", "h1", "xb"])
        self.af = Steps(sem("m_s_af"), ["bias0", "bias1"])

    def by_seq(self, t, seq):
        return t[seq].rearrange("h (a w) -> (h a) w", w=self.W)

    def load_constants(self, sp):
        for n, src in self.weights.items():
            sp.dma_start(self.w_sb[n][:, :, :], src.rearrange("(k p) n -> p k n", p=P)).then_inc(self.s_w, DMA)
        for n, src in self.columns.items():
            sp.dma_start(self.col[n][:, :], src).then_inc(self.s_w, DMA)
        sp.dma_start(self.bo_sb[:, :], self.bo.rearrange("(o c) -> o c", o=1).to_broadcast([P, C])
                     ).then_inc(self.s_w, DMA)

    def load_sums(self, sp, seq):
        sp.dma_start(self.den[:, seq, :], self.by_seq(self.den_d, seq)).then_inc(self.s_den[seq], DMA)

    def invert(self, dve, seq):
        dve.wait_ge(self.s_den[seq], DMA)
        dve.reciprocal(self.inv[:, seq, :], self.den[:, seq, :]).then_inc(self.s_inv, 1)

    def store_inverse(self, sp, seq):
        sp.wait_ge(self.s_inv, seq + 1)
        sp.dma_start(self.by_seq(self.rden_d, seq), self.inv[:, seq, :]).then_inc(self.s_rden[seq], DMA)

    def load(self, sp, blk, n):
        s = n % 2
        self.gf.wait(sp, blk - 2, "xb")
        self.ln.wait(sp, blk - 2, "x11")
        settle(sp, self.s_gate)
        tok = bass.ds(blk * TB, TB)
        for k in range(KH):
            sp.dma_start(self.num[s][:, k, :], self.num_d[k * P:(k + 1) * P, tok]).then_inc(self.s_in[s], DMA)
            for h in range(self.HH):
                sp.dma_start(self.rden[s][h * D:(h + 1) * D, k, :],
                             self.rden_d[blk // BPB, k * self.HH + h:k * self.HH + h + 1,
                                         bass.ds((blk % BPB) * TB, TB)].to_broadcast([D, TB])
                             ).then_inc(self.s_in[s], DMA)
            sp.dma_start(self.x_sb[s][:, 2 * k:2 * k + 2, :], self.x_v[blk, :, 2 * k:2 * k + 2, :]
                         ).then_inc(self.s_in[s], DMA)

    def heads(self, pool, blk, n):
        s = n % 2
        pool.wait_ge(self.s_in[s], DMA * self.N_IN * (blk // 2 + 1))
        for k in range(KH):
            self.pf.wait(pool, blk - 2, "proj")
            self.gf.done(pool.tensor_tensor(self.hT[s][:, k, :], self.num[s][:, k, :],
                                            self.rden[s][:, k, :], ALU.mult))
        self.gf.done(pool.tensor_tensor(self.x_sb[s][:, :, :], self.x_sb[s][:, :, :],
                                        self.bo_sb[:, :].unsqueeze(1).to_broadcast([P, TT, C]), ALU.add))

    def add_bias(self, ac, blk, n):
        for k in range(KH):
            self.gf.wait(ac, blk, f"h{k}")
            self.af.done(ac.activation(self.hT[n % 2][:, k, :], self.hT[n % 2][:, k, :], ACT.Identity,
                                       bias=self.col["bv"][:, k:k + 1]))


def stage_project(nc, psum, x, wqT, wkT, wvT, bq, bk, q_d, k_d, v_d, ahead):
    with ExitStack() as ctx:
        def sb(name, shape, dt):
            return ctx.enter_context(nc.sbuf_tensor(name, shape, dt))

        def sem(name):
            return ctx.enter_context(nc.semaphore(name))

        ident = sb("p_ident", [P, P], F32)
        w_sb = {n: sb(f"p_w{n}", [P, KH, C], F32) for n in "qkv"}
        bias = {n: sb(f"p_b{n}", [P, KH], F32) for n in "qk"}
        x_sb = [sb(f"p_x{s}", [P, TT, C], F32) for s in range(2)]
        xn = [sb(f"p_xn{s}", [P, TT, C], F32) for s in range(2)]
        xnT = [sb(f"p_xnT{s}", [P, KH, TB], F32) for s in range(2)]
        full = [sb(f"p_full{s}", [P, 4, TB], F32) for s in range(2)]
        rest = [sb(f"p_rest{s}", [P, 4, TB], F32) for s in range(2)]
        parts = [sb(f"p_parts{s}", [P, 4, PARTS, TB], BF16) for s in range(2)]
        v_sb = [sb(f"p_v{s}", [P, TT, C], F32) for s in range(2)]
        stats = sb("p_stats", [P, TT, 6], F32)
        mv = sb("p_mv", [P, TT, 2], F32)
        work = sb("p_work", [P, 5, TT], F32)

        s_w = sem("p_s_w")
        s_id = sem("p_s_id")
        s_gate = sem("p_s_gate")
        s_x = [sem(f"p_s_x{s}") for s in range(2)]
        s_wr = ahead.s_wr
        jobs = [("q", 0), ("q", 1), ("k", 0), ("k", 1)]
        ln = Steps(sem("p_s_ln"), LN_STEPS)
        pe = Steps(sem("p_s_pe"), [f"{n}{h}" for n, h in jobs] + ["v0", "v1"])
        pt = Steps(sem("p_s_pt"), ["turned0", "turned1"])
        act = Steps(sem("p_s_act"), ["xnT0", "xnT1"])
        av = Steps(sem("p_s_av"), [f"{s}{n}{h}" for n, h in jobs for s in ("full_", "part0_")] + ["v0", "v1"])
        spl = Steps(sem("p_s_spl"), [f"{s}{n}{h}" for n, h in jobs for s in ("rest_", "part1_")])
        least = Steps(sem("p_s_least"), [f"part2_{n}{h}" for n, h in jobs])

        x_v = x.rearrange("b (m t p) c -> (b m) p t c", p=P, t=TT)
        block = ctx.enter_context(nc.Block())

        @block.sync
        def _(sp):
            def load(s, blk):
                sp.dma_start(x_sb[s][:, :, :], x_v[blk, :, :, :]).then_inc(s_x[s], DMA)

            def store(s, blk):
                av.wait(sp, blk, "v1")
                settle(sp, s_gate)
                seq, tb = blk // BPB, blk % BPB
                for n in range(4):
                    sp.dma_start(v_d[seq * 4 + n, :, bass.ds(tb * TT, TT), :],
                                 v_sb[s][:, :, n * G * D:(n + 1) * G * D]).then_inc(s_wr[s], DMA)
                for j, (n, h) in enumerate(jobs):
                    least.wait(sp, blk, f"part2_{n}{h}")
                    settle(sp, s_gate)
                    dst = (q_d[blk, h] if n == "q" else
                           k_d[seq, h, :, :, bass.ds(tb * TB, TB)])
                    sp.dma_start(dst.rearrange("a p t -> p a t"), parts[s][:, j, :, :]).then_inc(s_wr[s], DMA)

            for s in range(2):
                sp.sem_inc(s_wr[s], DMA)
                load(s, s)
            for n, src in (("q", wqT), ("k", wkT), ("v", wvT)):
                sp.dma_start(w_sb[n][:, :, :], src.rearrange("(k p) n -> p k n", p=P)).then_inc(s_w, DMA)
            for n, src in (("q", bq), ("k", bk)):
                sp.dma_start(bias[n][:, :], src).then_inc(s_w, DMA)
            with sp.Fori(0, BLOCKS // 2 - 1) as turn:
                for s in range(2):
                    blk = turn * 2 + s
                    ln.wait(sp, blk, f"norm{TT - 1}")
                    settle(sp, s_gate)
                    load(s, blk + 2)
                    store(s, blk)
            for s in range(2):
                blk = BLOCKS - 2 + s
                av.wait(sp, blk - 1, "v1")
                settle(sp, s_gate)
                ahead.first(sp, s)
                store(s, blk)

        @block.gpsimd
        def _(pool):
            least.start(pool)
            make_identity(pool, ident, s_id)
            with pool.Fori(0, BLOCKS // 2) as turn:
                for s in range(2):
                    for j, (n, h) in enumerate(jobs):
                        spl.wait(pool, turn * 2 + s, f"part1_{n}{h}")
                        least.done(pool.tensor_tensor(parts[s][:, j, 2, :], rest[s][:, j, :],
                                                      parts[s][:, j, 1, :], ALU.subtract))

        @block.vector
        def _(dve):
            ln.start(dve)
            spl.start(dve)
            def norm(blk, s, turn):
                dve.wait_ge(s_x[s], DMA * (turn + 1))
                layernorm(dve, ln, blk, x_sb[s], xn[s], stats, mv, work)

            def pair(turn, last):
                for s in range(2):
                    blk = turn * 2 + s
                    if not (last and s):
                        norm(blk + 1, 1 - s, turn + s)
                    for j, (n, h) in enumerate(jobs):
                        av.wait(dve, blk, f"part0_{n}{h}")
                        spl.done(dve.tensor_tensor(rest[s][:, j, :], full[s][:, j, :],
                                                   parts[s][:, j, 0, :], ALU.subtract))
                        spl.wait(dve, blk, f"rest_{n}{h}")
                        spl.done(dve.tensor_copy(parts[s][:, j, 1, :], rest[s][:, j, :]))

            norm(0, 0, 0)
            with dve.Fori(0, BLOCKS // 2 - 1) as turn:
                pair(turn, False)
            pair(BLOCKS // 2 - 1, True)

        @block.tensor
        def _(te):
            pe.start(te)
            pt.start(te)
            te.wait_ge(s_id, 2)
            def turned(blk, s):
                act.wait(te, blk - 1, "xnT1")
                for t in range(TT):
                    ln.wait(te, blk, f"norm{t}")
                    for h in range(KH):
                        m = te.transpose(psum[:, h, t * P:(t + 1) * P], xn[s][:, t, h * P:(h + 1) * P],
                                         ident[:, :])
                        if t == TT - 1:
                            pt.done(m)

            def value(blk, s, half):
                av.wait(te, blk - 1, f"v{half}")
                for t in range(2 * half, 2 * half + 2):
                    o = psum[:, 6 + half, (t % 2) * C:(t % 2 + 1) * C]
                    for k in range(KH):
                        m = te.matmul(o, xnT[s][:, k, t * P:(t + 1) * P], w_sb["v"][:, k, :],
                                      start=(k == 0), stop=(k == KH - 1))
                pe.done(m)

            def pair(turn, last):
                for s in range(2):
                    blk = turn * 2 + s
                    act.wait(te, blk, "xnT1")
                    for j, (n, h) in enumerate(jobs):
                        av.wait(te, blk - 1, f"part0_{n}{h}")
                        for k in range(KH):
                            m = te.matmul(psum[:, 2 + j, :], w_sb[n][:, k, h * P:(h + 1) * P],
                                          xnT[s][:, k, :], start=(k == 0), stop=(k == KH - 1))
                        pe.done(m)
                    value(blk, s, 0)
                    if not (last and s):
                        turned(blk + 1, 1 - s)
                    value(blk, s, 1)

            turned(0, 0)
            te.wait_ge(s_w, DMA * 5)
            with te.Fori(0, BLOCKS // 2 - 1) as turn:
                pair(turn, False)
            pair(BLOCKS // 2 - 1, True)

        @block.scalar
        def _(ac):
            act.start(ac)
            av.start(ac)
            ac.wait_ge(s_w, DMA * 5)

            def keep_turned(blk, s):
                for h in range(KH):
                    pt.wait(ac, blk, f"turned{h}")
                    act.done(ac.copy(xnT[s][:, h, :], psum[:, h, :]))

            def keep_v(blk, s, half):
                pe.wait(ac, blk, f"v{half}")
                av.done(ac.copy(v_sb[s][:, 2 * half:2 * half + 2, :].rearrange("p t c -> p (t c)"),
                                psum[:, 6 + half, :]))

            def pair(turn, last):
                for s in range(2):
                    blk = turn * 2 + s
                    ac.wait_ge(s_wr[s], DMA * (STORES * turn + 1))
                    for j, (n, h) in enumerate(jobs):
                        pe.wait(ac, blk, f"{n}{h}")
                        av.done(ac.activation(full[s][:, j, :], psum[:, 2 + j, :], ACT.Identity,
                                              bias=bias[n][:, h:h + 1]))
                        av.done(ac.activation(parts[s][:, j, 0, :], psum[:, 2 + j, :], ACT.Identity,
                                              bias=bias[n][:, h:h + 1]))
                    keep_v(blk, s, 0)
                    if not (last and s):
                        keep_turned(blk + 1, 1 - s)
                    keep_v(blk, s, 1)

            keep_turned(0, 0)
            with ac.Fori(0, BLOCKS // 2 - 1) as turn:
                pair(turn, False)
            pair(BLOCKS // 2 - 1, True)


def stage_attend(nc, psum, num_d, den_d, inputs, ahead):
    LEAD = CH + 5
    AHEAD = LEAD - CH
    ST, O, RING = 0, 4, 5
    NRING, TURN_AT, TURN_KB = 3, CH - AHEAD + 2, 2
    IDLE = 6 * KB + 2
    SLOTS = CH * KB + 2
    FIRST = LEAD * KB + 2
    with ExitStack() as ctx:
        def sb(name, shape, dt):
            return ctx.enter_context(nc.sbuf_tensor(name, shape, dt))

        def sem(name):
            return ctx.enter_context(nc.semaphore(name))

        ks, qs, v_in = inputs.ks, inputs.qs, inputs.v_in
        v_st = sb("a_vst", [P, CH, G, 32], F32)
        p_sb = sb("a_p", [P, 2, G, TB], F32)
        o_sb = ahead.o_sb
        ident = sb("a_ident", [P, P], BF16)
        mx = sb("a_mx", [P, G * TT, KB], F32)
        m = sb("a_m", [P, G * TT], F32)
        m_rest = sb("a_mrest", [P, G * TT], F32)
        m_parts = sb("a_mparts", [P, PARTS, G * TT], BF16)
        m_rows = sb("a_mrows", [PARTS * G * TT, P], BF16)

        s_id = sem("a_s_id")
        s_one = sem("a_s_one")
        s_k, s_q, s_v = inputs.s_k, inputs.s_q, inputs.s_v
        s_vc = sem("a_s_vc")
        s_st = sem("a_s_st")
        s_exp = sem("a_s_exp")
        s_sp = sem("a_s_sp")
        s_mx = sem("a_s_mx")
        s_ch = sem("a_s_ch")
        s_mr = sem("a_s_mr")
        s_pv = sem("a_s_pv")
        s_oe = sem("a_s_oe")
        s_out = ahead.s_num
        s_te, s_gate = sem("a_s_te"), sem("a_s_gate")
        K_INC, Q_INC, V_INC = inputs.K_INC, inputs.Q_INC, inputs.V_INC
        M_INC, OUT_INC = DMA * PARTS, DMA * OUTPUTS
        CHAIN = 5

        def stream(it, c):
            late = c >= CH - AHEAD
            return it + 1 + late, (c + AHEAD) % CH

        TURN_TILE = TURN_AT * KB + TURN_KB
        TURN = TURN_TILE + 1

        def slot(it, n):
            return FIRST + SLOTS * it + n, RING + (FIRST + n) % NRING

        def tile(it, c, kb):
            n = c * KB + kb
            return slot(it, n + (n >= IDLE) + (n >= TURN_TILE))

        def taken(c, kb):
            return 1 + (c * KB + kb == IDLE - 1)

        SKIPPED = TURN_TILE - (CH - AHEAD) * KB
        BEFORE = range(-AHEAD, CH)

        block = ctx.enter_context(nc.Block())

        @block.sync
        def _(sp):
            def rows(it):
                sp.wait_ge(s_mx, NRING + slot(it - 1, TURN)[0] + 1)
                settle(sp, s_gate)
                for a in range(PARTS):
                    sp.dma_start(qs[SR + a:SR + a + 1, it % QRING, :].rearrange("o (n p) -> o n p", p=P),
                                 m_rows[a * G * TT:(a + 1) * G * TT, :]).then_inc(s_mr, DMA)

            def out(it):
                sp.wait_ge(s_oe, it + 2)
                settle(sp, s_gate)
                seq, grp, qb = it // (G * QB), (it // QB) % G, it % QB
                for g in range(G):
                    head, row = grp * G + g, 32 * g
                    sp.dma_start(num_d[bass.ds(head * D, D), bass.ds(seq * N + qb * TB, TB)],
                                 o_sb[row:row + D, :]).then_inc(s_out, DMA)
                    sp.dma_start(den_d[seq, bass.ds(head, 1), bass.ds(qb * TB, TB)],
                                 o_sb[row + D:row + D + 1, :]).then_inc(s_out, DMA)

            def body(it, k, q):
                sp.wait_ge(s_st, it * 2 * CH + 1)
                sp.wait_ge(s_vc, it * CH + CH)
                settle(sp, s_gate)
                if k:
                    inputs.load_k(sp, it + G)
                    inputs.load_v(sp, it + G)
                else:
                    sp.sem_inc(s_k, K_INC)
                    sp.sem_inc(s_v, V_INC)
                if q:
                    inputs.load_q(sp, it + QRING - 1)
                else:
                    sp.sem_inc(s_q, Q_INC)
                if not isinstance(it, int) or it + 1 < ITS:
                    rows(it + 1)
                sp.wait_ge(s_k, K_INC * (it + G + 1))
                settle(sp, s_gate)
                sp.wait_ge(s_v, V_INC * (it + G + 1))
                settle(sp, s_gate)
                sp.wait_ge(s_q, Q_INC * (it + QRING))
                settle(sp, s_gate)
                out(it)

            sp.sem_inc(s_out, DMA)
            sp.sem_inc(s_mr, DMA)
            for n in range(2, G):
                inputs.first(sp, n)
            for s in range(2):
                sp.wait_ge(inputs.s_wr[s], DMA * (STORES * (BLOCKS // 2) + 1))
            rows(0)
            with sp.Fori(0, ITS - G) as it:
                body(it, True, True)
            for it in range(ITS - G, ITS):
                if it == ITS - 2:
                    ahead.load_constants(sp)
                    for seq in range(B - 1):
                        ahead.load_sums(sp, seq)
                if it == ITS - 1:
                    for seq in range(B - 1):
                        ahead.store_inverse(sp, seq)
                    for n in range(2):
                        sp.wait_ge(ahead.s_rden[0], DMA)
                        ahead.load(sp, n, n)
                body(it, False, it + QRING - 1 < ITS)

        @block.gpsimd
        def _(pool):
            ahead.gf.start(pool)
            make_identity(pool, ident, s_id)
            pool.wait_ge(s_id, 2)
            pool.memset(v_st[:, :, :, :], 0.0).then_inc(s_one, 1)
            pool.wait_ge(s_one, 1)
            pool.memset(v_st[:, :, :, D:D + 1], 1.0).then_inc(s_one, 1)
            for u in range(2):
                pool.wait_ge(s_one, 2 + u)
                pool.memset(ks[SR:MR, u, :, :], 1.0).then_inc(s_one, 1)
            pool.wait_ge(s_one, 4)

            def copy_v(it, c):
                pool.tensor_copy(v_st[:, c, :, 0:D],
                                 v_in[:, (it // QB) % 2, c, :].rearrange("p (g d) -> p g d", g=G)
                                 ).then_inc(s_vc, 1)

            pool.wait_ge(s_v, V_INC * G)
            for c in range(CH):
                copy_v(0, c)
            with pool.Fori(0, ITS - 1) as it:
                for c in range(CH):
                    if c in (0, CH - CH // G):
                        pool.wait_ge(s_v, V_INC * (it + G + (c > 0)))
                    pool.wait_ge(s_pv, it * CH + c + 3)
                    copy_v(it + 1, c)
            pool.wait_ge(ahead.s_w, DMA * ahead.NW)
            for n in range(2):
                ahead.heads(pool, n, n)

        @block.scalar
        def _(ac):
            ac.sem_inc(s_exp, 2)
            ac.sem_inc(s_oe, 1)
            ahead.af.start(ac)

            def exp(it, c):
                ac.wait_ge(s_pv, it * CH + c + 1)
                for half in range(2):
                    ac.wait_ge(s_st, it * 2 * CH + 2 * c + half + 1)
                    ac.activation(p_sb[:, c % 2, 2 * half:2 * half + 2, :],
                                  psum[:, ST + 2 * half:ST + 2 * half + 2, :], ACT.Exp,
                                  scale=SCALE).then_inc(s_exp, 1)

            def keep_output(it):
                ac.wait_ge(s_pv, it * CH + CH + 2)
                ac.wait_ge(s_out, it * OUT_INC + DMA)
                ac.copy(o_sb[:, :], psum[:, O, :]).then_inc(s_oe, 1)

            exp(0, 0)
            with ac.Fori(0, ITS - 1) as it:
                for c in range(1, CH):
                    exp(it, c)
                exp(it + 1, 0)
                keep_output(it)
            for c in range(1, CH):
                exp(ITS - 1, c)
            ac.wait_ge(ahead.s_w, DMA * ahead.NW)
            ahead.add_bias(ac, 0, 0)
            keep_output(ITS - 1)

        @block.vector
        def _(dve):
            def chain(it, k):
                if k:
                    dve.wait_ge(s_ch, (it + 1) * CHAIN + k)
                else:
                    dve.wait_ge(s_mx, NRING + tile(it, CH - AHEAD - 1, KB - 1)[0] + 1)
                if k == 0:
                    ins = dve.tensor_reduce(m[:, :], mx[:, :, :], AX.X, ALU.max)
                elif k == 1:
                    ins = dve.tensor_scalar(m_parts[:, 0, :], m[:, :], -1.0, None, ALU.mult)
                elif k == 2:
                    ins = dve.scalar_tensor_tensor(out=m_rest[:, :], in0=m[:, :], scalar=-1.0,
                                                   in1=m_parts[:, 0, :], op0=ALU.mult, op1=ALU.subtract)
                elif k == 3:
                    ins = dve.tensor_copy(m_parts[:, 1, :], m_rest[:, :])
                else:
                    ins = dve.tensor_tensor(m_parts[:, 2, :], m_rest[:, :], m_parts[:, 1, :], ALU.subtract)
                ins.then_inc(s_ch, 1)

            def keep_rows(it):
                n, bank = slot(it, TURN)
                dve.wait_ge(s_sp, n + 1)
                dve.wait_ge(s_mr, M_INC * (it + 1) + DMA)
                dve.tensor_copy(m_rows[:, :], psum[0:PARTS * G * TT, bank, 0:P // 2].bitcast(BF16)
                                ).then_inc(s_mx, 1)

            def body(it, steps):
                for c in steps:
                    for kb in range(KB):
                        if (c, kb) == (TURN_AT, TURN_KB):
                            keep_rows(it)
                        n, bank = tile(it, c, kb)
                        if (c, kb) == (CH - AHEAD, 0):
                            dve.wait_ge(s_ch, (it + 1) * CHAIN + 1)
                        dve.wait_ge(s_sp, n + 1)
                        dve.tensor_reduce(mx[:, stream(it, c)[1], kb:kb + 1], psum[:, bank, :], AX.X, ALU.max
                                          ).then_inc(s_mx, taken(c, kb))
                        if c == CH - AHEAD:
                            chain(it, kb + 1)
                    if c == CH - AHEAD - 1:
                        chain(it, 0)

            ahead.ln.start(dve)
            body(-1, BEFORE)
            with dve.Fori(0, ITS - 2) as it:
                body(it, range(CH))
            body(ITS - 2, range(CH - AHEAD))
            for k in range(1, CHAIN):
                chain(ITS - 2, k)
            dve.wait_ge(s_sp, slot(ITS - 2, TURN)[0])
            dve.sem_inc(s_mx, SKIPPED)
            keep_rows(ITS - 2)
            for seq in range(B - 1):
                ahead.invert(dve, seq)

        @block.tensor
        def _(te):
            def scores(it, c, half):
                te.wait_ge(s_exp, it * 2 * CH + 2 * c + half + 1)
                for g in range(2 * half, 2 * half + 2):
                    mm = te.matmul(psum[:, ST + g, :], ks[0:MR, (it // QB) % 2, g, c * P:(c + 1) * P],
                                   qs[0:MR, it % QRING, g * TB:(g + 1) * TB], start=True, stop=True)
                mm.then_inc(s_st, 1)

            def peak(it, c, kbs):
                blk, pair = stream(it, c)
                for kb in kbs:
                    if (c, kb) == (TURN_AT, TURN_KB):
                        turn(it)
                    n, bank = tile(it, c, kb)
                    te.wait_ge(s_mx, n + 1)
                    te.matmul(psum[:, bank, :], qs[0:SR, blk % QRING, pair * P:(pair + 1) * P],
                              ks[0:SR, (blk // QB) % 2, pair // TT, kb * TB:(kb + 1) * TB],
                              start=True, stop=True).then_inc(s_sp, taken(c, kb))

            def turn(it):
                n, bank = slot(it, TURN)
                te.wait_ge(s_ch, CHAIN * (it + 2))
                te.wait_ge(s_mx, n + 1)
                settle(te, s_te)
                te.transpose(psum[0:PARTS * G * TT, bank, 0:P // 2].bitcast(BF16),
                             m_parts[:, :, :].rearrange("p a n -> p (a n)"), ident[:, :]).then_inc(s_sp, 1)

            def times_v(it, c):
                te.wait_ge(s_exp, it * 2 * CH + 2 * c + 4)
                te.wait_ge(s_vc, it * CH + c + 1)
                if c == 0:
                    te.wait_ge(s_oe, it + 1)
                for g in range(G):
                    mm = te.matmul(psum[32 * g:32 * g + 32, O, :], v_st[:, c, g, :],
                                   p_sb[:, c % 2, g, :], start=(c == 0), stop=(c == CH - 1))
                mm.then_inc(s_pv, 1)

            def steps(it, cs, peaks):
                for c in cs:
                    pair = stream(it, c)[1]
                    ahead = c < peaks
                    if c == 0:
                        te.wait_ge(s_mr, M_INC * (it + 1) + DMA)
                    if ahead and c == 0:
                        te.wait_ge(s_k, K_INC * (it + G))
                    if ahead and pair == 3 * TT:
                        te.wait_ge(s_k, K_INC * (it + G + 1))
                    if ahead and pair == 0:
                        te.wait_ge(s_q, Q_INC * (it + 3))
                    scores(it, c, 0)
                    if ahead:
                        peak(it, c, (0,))
                    scores(it, c, 1)
                    if ahead:
                        peak(it, c, (1,))
                    if c:
                        times_v(it, c - 1)
                    elif not isinstance(it, int) or it:
                        times_v(it - 1, CH - 1)
                    if ahead:
                        peak(it, c, (2, 3))
                    if c == TURN_AT and 0 < peaks < CH:
                        te.wait_ge(s_mx, NRING + slot(it, TURN)[0] - SKIPPED)
                        te.sem_inc(s_sp, SKIPPED)
                        turn(it)

            ahead.pf.start(te)
            te.sem_inc(s_pv, 2)
            te.sem_inc(s_mx, NRING)
            te.wait_ge(s_id, 2)
            te.wait_ge(s_q, Q_INC)
            for n in range(G):
                te.wait_ge(s_k, K_INC * (n + 1))
                for c in range(TT * n - AHEAD, TT * n + TT - AHEAD):
                    peak(-1, c, range(KB))
            te.wait_ge(s_one, 4)
            te.wait_ge(s_q, Q_INC * (QRING - 1))
            for c in range(CH - AHEAD, CH):
                peak(-1, c, range(KB))
            steps(0, range(1), CH)
            with te.Fori(0, ITS - 2) as it:
                steps(it, range(1, CH), CH)
                steps(it + 1, range(1), CH)
            steps(ITS - 2, range(1, CH), CH - AHEAD)
            steps(ITS - 1, range(CH), 0)
            times_v(ITS - 1, CH - 1)


def stage_mix(nc, psum, inputs, out):
    with ExitStack() as ctx:
        def sb(name, shape, dt):
            return ctx.enter_context(nc.sbuf_tensor(name, shape, dt))

        def sem(name):
            return ctx.enter_context(nc.semaphore(name))

        def two(name, shape):
            return [sb(f"m_{name}{s}", shape, F32) for s in range(2)]

        ident = sb("m_ident", [P, P], F32)
        w_sb, col, x_sb, hT = inputs.w_sb, inputs.col, inputs.x_sb, inputs.hT
        x1 = [sb(f"m_x1{n}", [P, TT, C], F32) for n in range(BPB)]
        xn = sb("m_xn", [P, TT, C], F32)
        xT = two("xT", [P, KH, TB + 1])
        diff = sb("m_diff", [P, KH, TB], F32)
        xr, xk = two("xr", [P, KH, TB]), two("xk", [P, KH, TB])
        kr, ka = sb("m_kr", [P, KH, TB], F32), sb("m_ka", [P, KH, TB], F32)
        gate = two("gate", [P, TT, C])
        y = two("y", [P, TT, C])
        stats = sb("m_stats", [P, TT, 6], F32)
        mv = sb("m_mv", [P, TT, 2], F32)
        work = sb("m_work", [P, 5, TT], F32)

        s_id, s_gate = sem("m_s_id"), inputs.s_gate
        s_out = [sem(f"m_s_out{s}") for s in range(2)]
        ln, pf, gf, af = inputs.ln, inputs.pf, inputs.gf, inputs.af
        pf_t = Steps(sem("m_s_pt"), ["turned0", "turned1"])
        pb_ = Steps(sem("m_s_pb"), ["k", "r", "v"])
        gb = Steps(sem("m_s_gb"), ["sq", "y"])
        at = Steps(sem("m_s_at"), ["xT0", "xT1"])
        ab = Steps(sem("m_s_ab"), ["relu", "gate"])
        vb = Steps(sem("m_s_vb"), ["prev", "diff", "xk0", "xk1", "xr0", "xr1"])
        vy = Steps(sem("m_s_vy"), ["gated"])

        out_v = out.rearrange("b (m t p) c -> (b m) p t c", p=P, t=TT)
        block = ctx.enter_context(nc.Block())

        def turns(eng, turn):
            with eng.Fori(0, B - 1) as seq:
                for n in range(BPB):
                    turn(seq * BPB + n, n)
            for n in range(BPB):
                turn((B - 1) * BPB + n, n)

        def there(blk):
            return not isinstance(blk, int) or blk < BLOCKS

        def uses(blk):
            return blk // 2

        @block.sync
        def _(sp):
            def back(blk, n):
                gb.wait(sp, blk, "y")
                settle(sp, s_gate)
                sp.dma_start(out_v[blk, :, :, :], y[n % 2][:, :, :]).then_inc(s_out[n % 2], DMA)

            for s in range(2):
                sp.sem_inc(s_out[s], DMA)
            def turn(blk, n):
                if there(blk + 3):
                    inputs.load(sp, blk + 3, n + 3)
                back(blk, n)

            sp.wait_ge(inputs.s_num, DMA * (OUTPUTS * ITS + 1))
            inputs.load_sums(sp, B - 1)
            for seq in range(1, B - 1):
                sp.wait_ge(inputs.s_rden[seq], DMA)
            inputs.load(sp, 2, 2)
            inputs.store_inverse(sp, B - 1)
            sp.wait_ge(inputs.s_rden[B - 1], DMA)
            turns(sp, turn)
            for s in range(2):
                sp.wait_ge(s_out[s], DMA * (BLOCKS // 2 + 1))

        @block.gpsimd
        def _(pool):
            gb.start(pool)
            make_identity(pool, ident, s_id)

            def turn(blk, n):
                s = n % 2
                ab.wait(pool, blk, "relu")
                pb_.wait(pool, blk - 1, "v")
                gb.done(pool.tensor_tensor(ka[:, :, :], kr[:, :, :], kr[:, :, :], ALU.mult))
                if there(blk + 2):
                    inputs.heads(pool, blk + 2, n + 2)
                vy.wait(pool, blk, "gated")
                gb.done(pool.tensor_tensor(y[s][:, :, :], y[s][:, :, :], x1[n % BPB][:, :, :], ALU.add))

            turns(pool, turn)

        @block.scalar
        def _(ac):
            for steps in (at, ab):
                steps.start(ac)

            def keep_turned(blk, n):
                for k in range(KH):
                    pf_t.wait(ac, blk, f"turned{k}")
                    vb.wait(ac, blk - 1, "prev")
                    at.done(ac.copy(xT[n % 2][:, k, 1:TB + 1], psum[:, 2 + k, :]))

            def turn(blk, n):
                s = n % 2
                pb_.wait(ac, blk, "k")
                gb.wait(ac, blk - 1, "sq")
                ab.done(ac.activation(kr[:, :, :], psum[:, 4:6, :], ACT.Relu))
                pb_.wait(ac, blk, "r")
                vy.wait(ac, blk - 2, "gated")
                ab.done(ac.activation(gate[s][:, :, :].rearrange("p t c -> p (t c)"),
                                      psum[:, 6:8, :].rearrange("p a c -> p (a c)"), ACT.Sigmoid))
                if there(blk + 1):
                    keep_turned(blk + 1, n + 1)
                if there(blk + 2):
                    inputs.add_bias(ac, blk + 2, n + 2)

            inputs.add_bias(ac, 1, 1)
            keep_turned(0, 0)
            turns(ac, turn)

        @block.vector
        def _(dve):
            for steps in (vb, vy):
                steps.start(dve)

            def front(blk, n):
                s = n % 2
                gf.wait(dve, blk, "xb")
                if n:
                    gb.wait(dve, blk - 3, "y")
                pf_t.wait(dve, blk - 1, "turned1")
                for b in range(2):
                    pf.wait(dve, blk, ("proj0", "proj")[b])
                    ln.done(dve.tensor_tensor(x1[n % BPB][:, 2 * b:2 * b + 2, :].rearrange("p t c -> p (t c)"),
                                              psum[:, b, :],
                                              x_sb[s][:, 2 * b:2 * b + 2, :].rearrange("p t c -> p (t c)"),
                                              ALU.add))
                layernorm(dve, ln, blk, x1[n % BPB], xn, stats, mv, work, ready=["x10", "x10", "x11", "x11"])
                at.wait(dve, blk, "xT1")
                if n % BPB == 0:
                    vb.done(dve.memset(xT[s][:, :, 0:1], 0.0))
                else:
                    vb.done(dve.tensor_copy(xT[s][:, :, 0:1], xT[1 - s][:, :, TB:TB + 1]))
                vb.wait(dve, blk, "prev")
                vb.done(dve.tensor_tensor(diff[:, :, :], xT[s][:, :, 1:TB + 1], xT[s][:, :, 0:TB],
                                          ALU.subtract))
                vb.wait(dve, blk, "diff")
                pb_.wait(dve, blk - 2, "r")
                for name, dst, mu in (("xk", xk, "mk"), ("xr", xr, "mr")):
                    for k in range(KH):
                        vb.done(dve.scalar_tensor_tensor(out=dst[s][:, k, :], in0=diff[:, k, :],
                                                         scalar=col[mu][:, k:k + 1], in1=xT[s][:, k, 0:TB],
                                                         op0=ALU.mult, op1=ALU.add))

            def back(blk, n):
                s = n % 2
                pb_.wait(dve, blk, "v")
                ab.wait(dve, blk, "gate")
                dve.wait_ge(s_out[s], DMA * (uses(blk) + 1))
                vy.done(dve.tensor_tensor(y[s][:, :, :].rearrange("p t c -> p (t c)"),
                                          psum[:, 4:6, :].rearrange("p a c -> p (a c)"),
                                          gate[s][:, :, :].rearrange("p t c -> p (t c)"), ALU.mult))

            def turn(blk, n):
                if there(blk + 1):
                    front(blk + 1, n + 1)
                back(blk, n)

            front(0, 0)
            inputs.invert(dve, B - 1)
            turns(dve, turn)

        @block.tensor
        def _(te):
            for steps in (pf_t, pb_):
                steps.start(te)

            def by_token(bank, lhsT, w, steps, halves=False):
                for t in range(TT):
                    for k in range(KH):
                        mm = te.matmul(psum[:, bank + t // 2, (t % 2) * C:(t % 2 + 1) * C],
                                       lhsT[:, k, t * P:(t + 1) * P], w[:, k, :],
                                       start=(k == 0), stop=(k == KH - 1))
                    if t == 1 and halves:
                        steps.done(mm)
                steps.done(mm)

            def proj(blk, n):
                af.wait(te, blk, "bias1")
                ln.wait(te, blk - 1, "x11")
                by_token(0, hT[n % 2], w_sb["o"], pf, halves=True)

            def turned(blk, n):
                at.wait(te, blk - 1, "xT1")
                for t in range(TT):
                    ln.wait(te, blk, f"norm{t}")
                    for h in range(KH):
                        mm = te.transpose(psum[:, 2 + h, t * P:(t + 1) * P], xn[:, t, h * P:(h + 1) * P],
                                          ident[:, :])
                        if t == TT - 1:
                            pf_t.done(mm)

            def products(blk, n):
                s = n % 2
                vb.wait(te, blk, "xk1")
                vy.wait(te, blk - 1, "gated")
                for h in range(KH):
                    for k in range(KH):
                        mm = te.matmul(psum[:, 4 + h, :], w_sb["k"][:, k, h * P:(h + 1) * P], xk[s][:, k, :],
                                       start=(k == 0), stop=(k == KH - 1))
                pb_.done(mm)
                vb.wait(te, blk, "xr1")
                ab.wait(te, blk - 1, "gate")
                by_token(6, xr[s], w_sb["r"], pb_)

            def value(blk, n):
                gb.wait(te, blk, "sq")
                by_token(4, ka, w_sb["v"], pb_)

            def turn(blk, n):
                if there(blk + 1):
                    proj(blk + 1, n + 1)
                products(blk, n)
                if there(blk + 1):
                    turned(blk + 1, n + 1)
                value(blk, n)

            proj(0, 0)
            te.wait_ge(s_id, 2)
            turned(0, 0)
            turns(te, turn)


def build(nc, a):
    dram = nc.dram_tensor
    q_d = dram("q_parts", (BLOCKS, KH, PARTS, P, TB), BF16).ap()
    k_d = dram("k_parts", (B, KH, PARTS, P, N), BF16).ap()
    v_d = dram("v_rows", (UNITS, P, CH, G * D), F32).ap()
    num_d = dram("numerators", (C, B * N), F32).ap()
    den_d = dram("denominators", (B, H, N), F32).ap()
    rden_d = dram("inverse_denominators", (B, H, N), F32).ap()
    with ExitStack() as ctx:
        psum = ctx.enter_context(nc.psum_tensor("psum", [P, 8, TB], F32))
        attend_inputs = AttendInputs(ctx, nc, q_d, k_d, v_d)
        mix_inputs = MixInputs(ctx, nc, a["x"], num_d, den_d, rden_d, a["bv"], a["woT"], a["bo"], a["fwrT"],
                               a["fwkT"], a["fwvT"], a["mu_r"], a["mu_k"])
        stage_project(nc, psum, a["x"], a["wqT"], a["wkT"], a["wvT"], a["bq"], a["bk"], q_d, k_d, v_d,
                      attend_inputs)
        stage_attend(nc, psum, num_d, den_d, attend_inputs, mix_inputs)
        stage_mix(nc, psum, mix_inputs, a["out"])


def kernel(L0_attn_x, L0_attn_Wq, L0_attn_bq, L0_attn_Wk, L0_attn_bk, L0_attn_Wv, L0_attn_bv,
           L0_attn_Wo, L0_attn_bo, L0_ffn_W_r, L0_ffn_W_k, L0_ffn_W_v, L0_ffn_mu_r, L0_ffn_mu_k):
    import concourse.bacc as bacc
    import numpy as np
    from concourse.bass_utils import run_bass_kernel_spmd

    turned = {"wqT": L0_attn_Wq, "wkT": L0_attn_Wk, "wvT": L0_attn_Wv, "woT": L0_attn_Wo,
              "fwrT": L0_ffn_W_r, "fwkT": L0_ffn_W_k, "fwvT": L0_ffn_W_v}
    arrays = {n: np.ascontiguousarray(np.asarray(w).T) for n, w in turned.items()}
    columns = {"bq": L0_attn_bq, "bk": L0_attn_bk, "bv": L0_attn_bv, "mu_r": L0_ffn_mu_r, "mu_k": L0_ffn_mu_k}
    arrays.update({n: np.ascontiguousarray(np.asarray(w).reshape(KH, P).T) for n, w in columns.items()})
    arrays.update(x=np.asarray(L0_attn_x), bo=np.asarray(L0_attn_bo))

    nc = bacc.Bacc("TRN2", target_bir_lowering=False, num_devices=1)
    a = {n: nc.dram_tensor(n, w.shape, mybir.dt.from_np(w.dtype), kind="ExternalInput").ap()
         for n, w in arrays.items()}
    a["out"] = nc.dram_tensor("out", (B, N, C), F32, kind="ExternalOutput").ap()
    build(nc, a)
    return run_bass_kernel_spmd(nc, [arrays], core_ids=[0]).results[0]["out"]
```
